# Optimizing a Trainium2 kernel written in Bass

```python
import numpy as np
import jax
import jax.numpy as jnp

def _softmax(x, axis=-1):
    return jax.nn.softmax(x, axis=axis)

def _gelu(x):
    return jax.nn.gelu(x, approximate=True)

def _silu(x):
    return jax.nn.silu(x)

def _sigmoid(x):
    return jax.nn.sigmoid(x)

def _layernorm(x, axis=-1, eps=1e-05):
    m = jnp.mean(x, axis=axis, keepdims=True)
    v = jnp.var(x, axis=axis, keepdims=True)
    return (x - m) / jnp.sqrt(v + eps)

def _scatter_add(tgt, idx, src, axis=0):
    return tgt.at[idx].add(src)

def _segment_sum(src, seg, n):
    return jax.ops.segment_sum(src, seg, n)
kernel_name = 'mk_gnn_resnorm_d2_gnn_r32_7c126a'

def setup_inputs(seed: int=0):
    np.random.seed(seed)
    _w = jnp.asarray

    def _rec_inputs():
        import jax
        import jax.numpy as jnp
        _gk = jax.random.key(seed)
        x = -0.000202 + 1 * jax.random.normal(jax.random.fold_in(_gk, 1), (3125, 128), jnp.float32)
        _s = jax.random.randint(jax.random.fold_in(_gk, 2), (25000,), 0, 3125, jnp.int32)
        _d = jax.random.randint(jax.random.fold_in(_gk, 3), (25000,), 0, 3125, jnp.int32)
        _loop = jnp.arange(3125, dtype=jnp.int32)
        src = jnp.concatenate([_s, _d, _loop])
        dst = jnp.concatenate([_d, _s, _loop])
        _o = jnp.argsort(dst, stable=True)
        src = src[_o]
        dst = dst[_o]
        edge_type_32 = jax.random.randint(jax.random.fold_in(_gk, 13), (53125,), 0, 32, jnp.int32)
        edge_weight1 = jax.random.uniform(jax.random.fold_in(_gk, 14), (53125, 1), jnp.float32, 0.0, 0.999998)
        return (x, src, dst, edge_type_32, edge_weight1)
    x, src, dst, edge_type_32, edge_weight1 = _rec_inputs()

    def _L0_gnn_setup():
        import jax, jax.numpy as jnp
        import numpy as np
        N_NODES = 50000
        N_EDGES = 25000
        IN_DIM = 128
        HID_DIM = 128
        BN_EPS = 1e-05
        key = jax.random.key(seed)
        ks = jax.random.split(key, 7)
        x = jax.random.normal(ks[0], (N_NODES, IN_DIM), dtype=jnp.float32)
        edge_index = jax.random.randint(ks[1], (2, N_EDGES), 0, N_NODES, dtype=jnp.int32)
        edge_attr = jax.random.uniform(ks[2], (N_EDGES, 1), dtype=jnp.float32)
        W = jax.random.normal(ks[3], (IN_DIM, HID_DIM), dtype=jnp.float32) / np.sqrt(IN_DIM)
        b = jnp.zeros((HID_DIM,), dtype=jnp.float32)
        gamma = jnp.ones((HID_DIM,), dtype=jnp.float32)
        beta = jnp.zeros((HID_DIM,), dtype=jnp.float32)
        return {'x': x, 'edge_index': edge_index, 'edge_attr': edge_attr, 'W': W, 'b': b, 'gamma': gamma, 'beta': beta}
    _L0_gnn_all = _L0_gnn_setup()
    _L0_gnn_in = {k: v for k, v in _L0_gnn_all.items() if k in ('W', 'b', 'gamma', 'beta')}
    del _L0_gnn_all

    def _L1_gnn_setup():
        import jax, jax.numpy as jnp
        import numpy as np
        N_NODES = 50000
        N_EDGES = 15625
        IN_FEAT = 128
        OUT_FEAT = 128
        NUM_RELS = 32
        NUM_BASES = 8
        key = jax.random.key(seed)
        ks = jax.random.split(key, 8)
        h = jax.random.normal(ks[0], (N_NODES, IN_FEAT), dtype=jnp.float32)
        src = jax.random.randint(ks[1], (N_EDGES,), 0, N_NODES, dtype=jnp.int32)
        dst = jax.random.randint(ks[2], (N_EDGES,), 0, N_NODES, dtype=jnp.int32)
        etype = jax.random.randint(ks[3], (N_EDGES,), 0, NUM_RELS, dtype=jnp.int32)
        norm = jax.random.uniform(ks[4], (N_EDGES, 1), dtype=jnp.float32)
        weight = jax.random.normal(ks[5], (NUM_BASES, IN_FEAT, OUT_FEAT), dtype=jnp.float32) * 0.05
        w_comp = jax.random.normal(ks[6], (NUM_RELS, NUM_BASES), dtype=jnp.float32) * 0.3
        bias_param = jax.random.normal(ks[7], (OUT_FEAT,), dtype=jnp.float32) * 0.05
        return {'h': h, 'src': src, 'dst': dst, 'etype': etype, 'norm': norm, 'weight': weight, 'w_comp': w_comp, 'bias_param': bias_param}
    _L1_gnn_all = _L1_gnn_setup()
    _L1_gnn_in = {k: v for k, v in _L1_gnn_all.items() if k in ('weight', 'w_comp', 'bias_param')}
    del _L1_gnn_all
    return {'x': x, 'src': src, 'dst': dst, 'edge_type_32': edge_type_32, 'edge_weight1': edge_weight1, 'L0_gnn_W': _L0_gnn_in['W'], 'L0_gnn_b': _L0_gnn_in['b'], 'L0_gnn_gamma': _L0_gnn_in['gamma'], 'L0_gnn_beta': _L0_gnn_in['beta'], 'L1_gnn_weight': _L1_gnn_in['weight'], 'L1_gnn_w_comp': _L1_gnn_in['w_comp'], 'L1_gnn_bias_param': _L1_gnn_in['bias_param']}

def reference(x, src, dst, edge_type_32, edge_weight1, L0_gnn_W, L0_gnn_b, L0_gnn_gamma, L0_gnn_beta, L1_gnn_weight, L1_gnn_w_comp, L1_gnn_bias_param):
    import jax
    import jax.numpy as jnp

    def _L0_gnn_ref(x, edge_index, edge_attr, W, b, gamma, beta):
        import jax, jax.numpy as jnp
        import numpy as np
        N_NODES = 50000
        N_EDGES = 25000
        IN_DIM = 128
        HID_DIM = 128
        BN_EPS = 1e-05
        n = x.shape[0]
        loop = jnp.arange(n, dtype=edge_index.dtype)
        src = jnp.concatenate([edge_index[0], loop])
        dst = jnp.concatenate([edge_index[1], loop])
        deg = jax.ops.segment_sum(jnp.ones_like(dst, dtype=x.dtype), dst, num_segments=n)
        dinv = jnp.where(deg > 0, jax.lax.rsqrt(deg), 0.0)
        norm = dinv[src] * dinv[dst]
        h = x @ W
        msg = h[src] * norm[:, None]
        agg = jax.ops.segment_sum(msg, dst, num_segments=n) + b
        y = jax.nn.relu(agg)
        mean = jnp.mean(y, axis=0)
        var = jnp.var(y, axis=0)
        return gamma * (y - mean) * jax.lax.rsqrt(var + BN_EPS) + beta

    def _L1_gnn_ref(h, src, dst, etype, norm, weight, w_comp, bias_param):
        import jax, jax.numpy as jnp
        import numpy as np
        N_NODES = 50000
        N_EDGES = 15625
        IN_FEAT = 128
        OUT_FEAT = 128
        NUM_RELS = 32
        NUM_BASES = 8
        hsrc = h[src]
        coef = w_comp[etype]
        msg = jnp.zeros((hsrc.shape[0], weight.shape[2]), dtype=h.dtype)
        for b in range(weight.shape[0]):
            msg = msg + hsrc @ weight[b] * coef[:, b][:, None]
        msg = msg * norm
        node_repr = jax.ops.segment_sum(msg, dst, num_segments=h.shape[0])
        node_repr = node_repr + bias_param
        return jax.nn.relu(node_repr)
    edge_index = jnp.stack([src, dst])
    x = _layernorm(x + _L0_gnn_ref(x, edge_index, edge_weight1, L0_gnn_W, L0_gnn_b, L0_gnn_gamma, L0_gnn_beta), axis=-1)
    x = _layernorm(x + _L1_gnn_ref(x, src, dst, edge_type_32, edge_weight1, L1_gnn_weight, L1_gnn_w_comp, L1_gnn_bias_param), axis=-1)
    return x

_drawn_inputs = setup_inputs


def setup_inputs(seed=0):
    import zlib

    import numpy as np

    out = dict(_drawn_inputs(seed))
    spreads = {'L0_gnn_b': (0.0, 0.1), 'L0_gnn_gamma': (1.0, 0.2), 'L0_gnn_beta': (0.0, 0.1)}
    factors = {}
    for name, (base, spread) in spreads.items():
        noise = np.random.default_rng([zlib.crc32(name.encode()), seed]).standard_normal(out[name].shape)
        drawn = base * np.exp(spread * noise) if base else spread * noise
        out[name] = jnp.asarray(drawn.astype(out[name].dtype))
    for name, factor in factors.items():
        out[name] = (out[name] * factor).astype(out[name].dtype)
    return out
```

```python
from contextlib import ExitStack

import concourse.bass as bass
import numpy as np
from concourse import mybir

F32 = mybir.dt.float32
BF16 = mybir.dt.bfloat16
FP16 = mybir.dt.float16
I32 = mybir.dt.int32
ALU = mybir.AluOpType
ACT = mybir.ActivationFunctionType
AX_X = mybir.AxisListType.X

P = 128
EPS = 1e-5


def gnn_kernel(nc, x, src, dst, etype, eweight, w0, b0, gamma, beta, w1, wcomp, b1, out, x1_dram):
    N, D = x.shape
    E = src.shape[0]
    K = w1.shape[0]
    R = wcomp.shape[0]
    assert D == P
    TILES = -(-E // P)
    UNIT = 32
    TILES = -(-TILES // UNIT) * UNIT
    HB = -(-N // P)
    NTAIL = N - (HB - 1) * P
    NPAD = HB * P
    WIN = 12
    LAST_BASE = NPAD - WIN
    PASSES = -(-N // WIN) + 1
    KEYS = HB * WIN
    BATCH = 16
    NB = TILES // BATCH
    BW = BATCH * WIN
    TG = -(-TILES // P)
    TLAST = TILES - (TG - 1) * P
    FULL_ROWS = E // P - (TG - 1) * P
    REST = E % P
    HALF = 8
    RING = 2 * HALF
    GROUPS = P // R
    GT = TILES // GROUPS
    CT = 13
    CHUNKS = GT // CT
    assert GT % CT == 0 and CT * GROUPS * K <= 512 and TLAST == 32 and 0 < REST

    with ExitStack() as ctx:
        def sb(name, shape, dt):
            return ctx.enter_context(nc.sbuf_tensor(name, shape, dt))

        def ps(name, shape, dt=F32):
            return ctx.enter_context(nc.psum_tensor(name, shape, dt))

        def sem(name):
            return ctx.enter_context(nc.semaphore(name))

        ident = sb("ident", [P, P], F32)
        ones = sb("ones", [P, P], F32)
        iota_row = sb("iota_row", [P, P], FP16)
        iota_keys = sb("iota_keys", [P, KEYS], FP16)
        iota_blk = sb("iota_blk", [P, HB], F32)
        iota_win = sb("iota_win", [P, WIN], F32)
        win_ends = sb("win_ends", [1, PASSES], F32)
        part_id = sb("part_id", [P, 1], I32)
        rel_id = sb("rel_id", [P, 1], F32)
        X = sb("X", [P, HB, D], F32)
        W0 = sb("W0", [P, D], F32)
        W1 = sb("W1", [P, K, D], F32)
        b0_all = sb("b0_all", [P, D], F32)
        gamma_all = sb("gamma_all", [P, D], F32)
        beta_all = sb("beta_all", [P, D], F32)
        b1_all = sb("b1_all", [P, D], F32)
        wblk = sb("wblk", [P, GROUPS, K], F32)
        ew_t = sb("ew_t", [P, TG, P], F32)
        base_t = sb("base_t", [P, TG], F32)
        max_t = sb("max_t", [P, TG], F32)
        rel = sb("rel", [P, TILES], F32)
        relw = sb("relw", [P, TILES], F32)
        ew = sb("ew", [P, TILES], F32)
        src_i = sb("src_i", [P, TILES], I32)
        ohw = sb("ohw", [P, TILES, WIN], BF16)
        zeros = sb("zeros", [P, P], BF16)
        base_row0 = sb("base_row0", [1, TG * P], F32)
        coef = sb("coef", [P, TILES, K], F32)
        base_row = sb("base_row", [1, TG * P], F32)
        span_row = sb("span_row", [1, TG * P], F32)
        base_i = sb("base_i", [1, TG * P], I32)
        span_max = sb("span_max", [1, 1], F32)
        npass_f = sb("npass_f", [1, 1], F32)
        npass_i = sb("npass_i", [1, 1], I32)
        dinv = sb("dinv", [P, HB], F32)
        Xs = sb("Xs", [P, HB, D], F32)
        OHS = 2 * BATCH
        stage0 = sb("stage0", [P, 2, 2, BATCH], F32)
        sums_all = sb("sums", [P, K * NPAD], F32)
        sums = sums_all[:, :].rearrange("p (k n) -> p k n", k=K)
        sum0 = sums_all[:, 0:NPAD]

        def inside(at, dt, *dims, space=sums_all, size=K * NPAD):
            words = -(-int(np.prod(dims)) * (4 if dt in (F32, I32) else 2) // 4)
            assert at + words <= size
            names = "abcd"[:len(dims)]
            view = space[:, at:at + words].bitcast(dt).rearrange(
                f"p ({' '.join(names)}) -> p {' '.join(names)}", **dict(zip(names, dims)))
            return view, at + words

        at = NPAD
        Xp = []
        for _ in range(3):
            part, at = inside(at, BF16, HB, D)
            Xp.append(part)
        counts, at = inside(at, BF16, 2, HB, BW)
        types, at = inside(at, I32, CT * P)
        oh_type, at = inside(at, F32, CT * P)
        dst_ti, at = inside(at, I32, TG, P)
        src_ti, at = inside(at, I32, TG, P)
        dst_t, at = inside(at, F32, TG, P)
        src_t, at = inside(at, F32, TG, P)
        rel_t, at = inside(at, F32, TG, P)
        hist_at = at
        oh_src, at = inside(at, BF16, OHS, P)
        oh_key, at = inside(at, BF16, OHS, KEYS)
        hist_lo, at = inside(hist_at, BF16, 16, P)
        oh_blk, at = inside(at, BF16, TILES, HB)
        idx = sb("idx", [P, 2, HALF], I32)
        ring_words = RING * D + RING * K * WIN
        rings = sb("rings", [P, ring_words], F32)
        G, at = inside(0, F32, RING, D, space=rings, size=ring_words)
        S, at = inside(at, F32, RING, K, WIN, space=rings, size=ring_words)
        keylo, at = inside(0, F32, 2, TILES, space=rings, size=ring_words)
        src_hi, at = inside(at, F32, TILES, space=rings, size=ring_words)
        valid, at = inside(at, F32, TILES, space=rings, size=ring_words)
        int_a, at = inside(at, I32, TILES, space=rings, size=ring_words)
        dst_lo, at = inside(at, F32, TILES, space=rings, size=ring_words)
        dst_hi, at = inside(at, F32, TILES, space=rings, size=ring_words)
        stats = sb("stats", [P, HB, 6], F32)
        mv = sb("mv", [P, HB, 2], F32)
        rstd = sb("rstd", [P, HB], F32)
        bn_a = sb("bn_a", [P, D], F32)
        bn_b = sb("bn_b", [P, D], F32)
        eps_c = sb("eps_c", [P, 1], F32)
        Y = sb("Y", [P, HB, D], F32)

        ring_ps = [ps(f"ring_ps{i}", [P, 512]) for i in range(4)]
        z_ps = [ps(f"z_ps{i}", [P, 512]) for i in range(2)]
        misc = [ps(f"misc{i}", [P, 512]) for i in range(2)]

        s_iota = sem("s_iota")
        s_const = sem("s_const")
        s_pad = sem("s_pad")
        s_ldst = sem("s_ldst")
        s_lsrc = sem("s_lsrc")
        s_lew = sem("s_lew")
        s_lx = sem("s_lx")
        s_lw = sem("s_lw")
        s_types = sem("s_types")
        s_dve = sem("s_dve")
        s_tr = sem("s_tr")
        s_tab = sem("s_tab")
        s_prep = sem("s_prep")
        s_hist = sem("s_hist")
        s_histmm = sem("s_histmm")
        s_oht = sem("s_oht")
        s_cmm = sem("s_cmm")
        s_cev = sem("s_cev")
        s_deg = sem("s_deg")
        s_act = sem("s_act")
        s_xs = sem("s_xs")
        s_xT = sem("s_xT")
        s_xTc = sem("s_xTc")
        s_key = sem("s_key")
        s_stage0 = sem("s_stage0")
        s_oh = sem("s_oh")
        s_cnt_mm = sem("s_cnt_mm")
        s_cnt = sem("s_cnt")
        s_z = sem("s_z")
        s_zadd = sem("s_zadd")
        s_zself = sem("s_zself")
        s_turn = sem("s_turn")
        s_y = sem("s_y")
        s_yev = sem("s_yev")
        s_bn = sem("s_bn")
        s_x1 = sem("s_x1")
        s_x1st = sem("s_x1st")
        s_stage1 = sem("s_stage1")
        s_g = [sem(f"s_g{i}") for i in range(RING)]
        s_S = sem("s_S")
        s_mm = sem("s_mm")
        s_add = sem("s_add")
        s_fin = sem("s_fin")
        s_fev = sem("s_fev")
        s_outr = sem("s_outr")
        s_out = sem("s_out")
        s_ohw = sem("s_ohw")
        s_zero = sem("s_zero")

        def passes(eng):
            eng.wait_ge(s_prep, 1)
            return eng.value_load(npass_i[0:1, 0:1], min_val=1, max_val=PASSES)

        def block_rows(h):
            return P if h < HB - 1 else NTAIL

        def edges_by_tile(a):
            full = (TG - 1) * P * P
            return (a[0:full].rearrange("(g t p) -> t g p", t=P, p=P),
                    a[full:full + FULL_ROWS * P].rearrange("(t p) -> t p", p=P),
                    a[full + FULL_ROWS * P:E].rearrange("(t p) -> t p", t=1))

        block = ctx.enter_context(nc.Block())

        @block.sync
        def _(sp):
            def load_edges(tile, a, signal):
                main, rows, rest = edges_by_tile(a)
                sp.dma_start(tile[:, 0:TG - 1, :], main).then_inc(signal, 16)
                sp.dma_start(tile[0:FULL_ROWS, TG - 1, :], rows).then_inc(signal, 16)
                sp.dma_start(tile[FULL_ROWS:FULL_ROWS + 1, TG - 1, 0:REST], rest).then_inc(signal, 16)

            sp.wait_ge(s_pad, 1)
            load_edges(dst_ti, dst, s_ldst)
            load_edges(src_ti, src, s_lsrc)
            load_edges(ew_t, eweight.rearrange("e o -> (e o)"), s_lew)
            for c in range(CHUNKS):
                if c == 0:
                    sp.wait_ge(s_pad, 2)
                else:
                    sp.wait_ge(s_oht, c)
                for g in range(GROUPS):
                    e0 = (g * GT + c * CT) * P
                    n = min(CT * P, E - e0)
                    sp.dma_start(types[g * R:(g + 1) * R, 0:n],
                                 etype[e0:e0 + n].partition_broadcast(R)).then_inc(s_types, 16)
            sp.wait_ge(s_x1, 1)
            sp.dma_start(x1_dram[0:(HB - 1) * P, :].rearrange("(h p) f -> p h f", p=P),
                         Xs[:, 0:HB - 1, :]).then_inc(s_x1st, 16)
            sp.dma_start(x1_dram[(HB - 1) * P:N, :], Xs[0:NTAIL, HB - 1, :]).then_inc(s_x1st, 16)
            for h in range(HB):
                sp.wait_ge(s_outr, h + 1)
                n = block_rows(h)
                sp.dma_start(out[h * P:h * P + n, :], Y[0:n, h, :]).then_inc(s_out, 16)
            sp.wait_ge(s_out, 16 * HB)

        @block.gpsimd
        def _(pool):
            g = nc.gpsimd
            g.memset(dst_ti[:, TG - 1, :], -1)
            g.memset(src_ti[:, TG - 1, :], 0)
            g.memset(ew_t[:, TG - 1, :], 0.0).then_inc(s_pad, 1)
            g.memset(types[:, :], 0).then_inc(s_pad, 1)
            g.memset(X[:, HB - 1, :], 0.0)
            g.memset(wblk[:, :, :], 0.0).then_inc(s_pad, 1)
            g.memset(ones[:, :], 1.0)
            g.memset(zeros[:, :], 0.0)
            g.memset(ident[:, :], 0.0).then_inc(s_iota, 1)
            pool.wait_ge(s_iota, 1)
            g.affine_select(out=ident[:, :], in_=ident[:, :], compare_op=ALU.not_equal, fill=1.0, base=0,
                            pattern=[[-1, P]], channel_multiplier=1)
            g.memset(eps_c[:, :], EPS)
            imprecise = dict(allow_small_or_imprecise_dtypes=True)
            g.iota(iota_row[:, :], [[1, P]], base=0, channel_multiplier=0, **imprecise)
            g.iota(iota_keys[:, :], [[1, KEYS]], base=1, channel_multiplier=0, **imprecise)
            g.iota(iota_blk[:, :], [[1, HB]], base=0, channel_multiplier=0, **imprecise)
            g.iota(iota_win[:, :], [[1, WIN]], base=0, channel_multiplier=0, **imprecise)
            g.iota(win_ends[:, :], [[WIN, PASSES]], base=WIN, channel_multiplier=0, **imprecise)
            g.iota(part_id[:, :], [[0, 1]], base=0, channel_multiplier=1).then_inc(s_const, 1)

            n_pass = passes(pool)
            with pool.Fori(0, n_pass) as w:
                pool.wait_ge(s_key, w + 1)
                pool.sem_inc(s_turn)
                with pool.Fori(0, NB // 2) as i:
                    for b in range(2):
                        m = w * NB + i * 2 + b
                        pool.wait_ge(s_oh, (m + 1) * BATCH)
                        g.tensor_copy(stage0[:, b, :, :],
                                      keylo[:, :, bass.ds((i * 2 + b) * BATCH, BATCH)]).then_inc(s_stage0, 1)

            pool.wait_ge(s_zself, n_pass * TILES + 1)
            pool.sem_inc(s_turn)
            g.memset(sums_all[:, NPAD:], 0.0)
            pool.wait_ge(s_y, HB)
            g.memset(sum0, 0.0).then_inc(s_zero, 1)
            pool.wait_ge(s_x1st, 32)
            with pool.Fori(0, n_pass) as w:
                with pool.Fori(0, TILES // RING) as i:
                    for b in range(2):
                        pool.wait_ge(s_stage1, w * (TILES // HALF) + i * 2 + b + 1)
                        pool.sem_inc(s_turn)
                        for j in range(HALF):
                            q = b * HALF + j
                            g.indirect_dma_start(G[:, q, :], None, x1_dram[:, :],
                                                 bass.IndirectOffsetOnAxis(ap=idx[:, b, j:j + 1], axis=0)
                                                 ).then_inc(s_g[q], 16)

        @block.scalar
        def _(act):
            a = nc.scalar
            act.dma_start(X[:, 0:HB - 1, :],
                          x[0:(HB - 1) * P, :].rearrange("(h p) f -> p h f", p=P)).then_inc(s_lx, 16)
            act.dma_start(W0[:, :], w0).then_inc(s_lw, 16)
            act.dma_start(W1[:, :, :], w1.rearrange("k f o -> f k o")).then_inc(s_lw, 16)
            for vec, tile in ((b0, b0_all), (gamma, gamma_all), (beta, beta_all), (b1, b1_all)):
                act.dma_start(tile[:, :], vec.partition_broadcast(P)).then_inc(s_lw, 16)
            act.wait_ge(s_pad, 3)
            act.dma_start(X[0:NTAIL, HB - 1, :], x[(HB - 1) * P:N, :]).then_inc(s_lx, 16)
            for g in range(GROUPS):
                act.dma_start(wblk[g * R:(g + 1) * R, g, :], wcomp).then_inc(s_lw, 16)

            act.wait_ge(s_histmm, TILES + 16)
            a.activation(dinv[:, :], misc[1][:, 0:HB], ACT.Sqrt, bias=ones[:, 0:1]).then_inc(s_deg, 1)
            act.wait_ge(s_xs, 1)
            a.copy(Xp[0][:, :, :], Xs[:, :, :]).then_inc(s_act, 1)
            act.wait_ge(s_xs, 2)
            a.copy(Xp[1][:, :, :], Y[:, :, :]).then_inc(s_act, 1)
            for q in range(-(-HB // 4)):
                n = min(4, HB - 4 * q)
                act.wait_ge(s_xT, q + 1)
                a.copy(sum0[:, 4 * q * P:(4 * q + n) * P], z_ps[q % 2][:, 0:n * P]).then_inc(s_xTc, 1)

            act.sem_inc(s_cnt, 4)
            n_pass = passes(act)
            with act.Fori(0, n_pass) as w:
                with act.Fori(0, NB // 2) as i:
                    for b in range(2):
                        m = w * NB + i * 2 + b
                        act.wait_ge(s_z, m + 1)
                        for j in range(BATCH):
                            act.wait_ge(s_cnt_mm, m * BATCH + (OHS + j + 1))
                            a.copy(counts[:, b, :, j * WIN:(j + 1) * WIN],
                                   ring_ps[j % 4][:, 0:KEYS].rearrange("p (h j) -> p h j", j=WIN)
                                   ).then_inc(s_cnt, 1)

            for q in range(-(-HB // 4)):
                n = min(4, HB - 4 * q)
                act.wait_ge(s_yev, 4 * q + n)
                a.activation(Y[:, 4 * q:4 * q + n, :], Y[:, 4 * q:4 * q + n, :], ACT.Relu).then_inc(s_act, 1)
            n_act = 2 + -(-HB // 4)
            act.wait_ge(s_bn, 1)
            a.activation(Xs[:, :, :], Y[:, :, :], ACT.Square).then_inc(s_act, 1)
            act.wait_ge(s_bn, 2)
            a.activation(bn_b[:, :], misc[1][:, 0:D], ACT.Sqrt, bias=eps_c[:, :], scale=1.0 / N).then_inc(s_act, 1)
            act.wait_ge(s_bn, 3)
            a.activation(rstd[:, :], mv[:, :, 1], ACT.Sqrt, bias=eps_c[:, :]).then_inc(s_act, 1)

            with act.Fori(0, n_pass) as w:
                with act.Fori(0, TILES // RING) as i:
                    for b in range(2):
                        t0 = i * RING + b * HALF
                        act.wait_ge(s_mm, w * TILES + t0 + HALF)
                        a.copy(idx[:, b, :], src_i[:, bass.ds(t0, HALF)]).then_inc(s_stage1, 1)
            for h in range(HB):
                act.wait_ge(s_fev, h + 1)
                a.activation(rstd[:, h:h + 1], mv[:, h, 1:2], ACT.Sqrt, bias=eps_c[:, :]).then_inc(s_act, 1)

        @block.tensor
        def _(pe):
            t = nc.tensor
            pe.wait_ge(s_const, 1)
            pe.wait_ge(s_tab, 1)
            for k, col in ((0, base_t), (1, max_t)):
                for g in range(TG):
                    last = t.matmul(misc[k][0:1, g * P:(g + 1) * P], col[:, g:g + 1], ident[:, :],
                                    start=True, stop=True)
            last.then_inc(s_tr, 1)
            pe.wait_ge(s_lew, 48)
            for k, by_tile in enumerate((rel_t, src_t, dst_t, ew_t)):
                for g in range(TG):
                    n = P if g < TG - 1 else TLAST
                    last = t.transpose(ring_ps[k][:, g * P:g * P + n], by_tile[0:n, g, :], ident[0:n, 0:n])
                last.then_inc(s_tr, 1)
            pe.wait_ge(s_tab, 2)
            t.matmul(misc[1][:, 0:HB], zeros[:, :], zeros[:, 0:HB], start=True, stop=False,
                     skip_group_check=True)
            pe.sem_inc(s_histmm, 16)
            with pe.Fori(0, TILES // 16) as i:
                for j in range(16):
                    pe.wait_ge(s_hist, i * 16 + (16 + j + 1))
                    t.matmul(misc[1][:, 0:HB], hist_lo[:, j, :], oh_blk[:, bass.ds(i * 16 + j, 1), :],
                             start=False, stop=False, skip_group_check=True).then_inc(s_histmm, 1)
            pe.wait_ge(s_lw, 16 * (6 + GROUPS))
            for c in range(CHUNKS):
                pe.wait_ge(s_oht, c + 1)
                if c >= 1:
                    pe.wait_ge(s_cev, c)
                for j in range(CT):
                    last = t.matmul(misc[0][:, j * GROUPS * K:(j + 1) * GROUPS * K],
                                    oh_type[:, j * P:(j + 1) * P], wblk[:, :, :].rearrange("p g k -> p (g k)"),
                                    start=True, stop=True)
                last.then_inc(s_cmm, 1)
            pe.wait_ge(s_xs, 1)
            for q in range(-(-HB // 4)):
                if q >= 2:
                    pe.wait_ge(s_xTc, q - 1)
                for j in range(min(4, HB - 4 * q)):
                    last = t.transpose(z_ps[q % 2][:, j * P:(j + 1) * P], Xs[:, 4 * q + j, :], ident[:, :])
                last.then_inc(s_xT, 1)
            pe.wait_ge(s_xTc, -(-HB // 4))

            pe.sem_inc(s_cnt_mm, OHS)
            pe.sem_inc(s_z, 2)
            pe.sem_inc(s_mm, RING)

            def count(m, b, js=range(BATCH)):
                for j in js:
                    pe.wait_ge(s_oh, m * BATCH + (OHS + j + 1))
                    pe.wait_ge(s_cnt, m * BATCH + (j + 1))
                    t.matmul(ring_ps[j % 4][:, 0:KEYS], oh_src[:, b * BATCH + j, :],
                             oh_key[:, b * BATCH + j, :], start=True, stop=True).then_inc(s_cnt_mm, 1)

            def aggregate(m, b):
                pe.wait_ge(s_cnt, m * BATCH + (4 + BATCH))
                pe.wait_ge(s_zadd, m + 1)
                for h in range(HB):
                    for k in range(3):
                        last = t.matmul(z_ps[b][:, 0:BW], Xp[k][:, h, :], counts[:, b, h, :],
                                        start=(h == 0 and k == 0), stop=(h == HB - 1 and k == 2))
                last.then_inc(s_z, 1)

            n_pass = passes(pe)
            pe.wait_ge(s_act, 2)
            pe.wait_ge(s_xs, 3)
            with pe.Fori(0, n_pass) as w:
                count(w * NB, 0)
                with pe.Fori(0, NB // 2 - 1) as i:
                    m = w * NB + i * 2
                    count(m + 1, 1)
                    aggregate(m, 0)
                    count(m + 2, 0)
                    aggregate(m + 1, 1)
                m = w * NB + (NB - 2)
                count(m + 1, 1)
                aggregate(m, 0)
                aggregate(m + 1, 1)

            pe.wait_ge(s_zself, n_pass * TILES + 1)
            for h in range(HB):
                if h >= 4:
                    pe.wait_ge(s_yev, h - 3)
                t.matmul(ring_ps[h % 4][:, 0:D], sum0[:, h * P:(h + 1) * P], W0[:, :],
                         start=True, stop=True).then_inc(s_y, 1)
            for k in range(2):
                vals = Y if k == 0 else Xs
                if k == 1:
                    pe.wait_ge(s_act, 2 + -(-HB // 4) + 1)
                for h in range(HB):
                    if k == 0:
                        pe.wait_ge(s_act, 2 + h // 4 + 1)
                    n = block_rows(h)
                    last = t.matmul(misc[k][:, 0:D], ones[0:n, :], vals[0:n, h, :], start=(h == 0), stop=(h == HB - 1))
                last.then_inc(s_y, 1)

            with pe.Fori(0, n_pass) as w:
                with pe.Fori(0, TILES // RING) as i:
                    for j in range(RING):
                        done = w * TILES + i * RING + (j + 1)
                        if j % HALF == 0:
                            pe.wait_ge(s_S, (w * (TILES // RING) + i) * 2 + (j // HALF + 1))
                        pe.wait_ge(s_add, done)
                        pe.wait_ge(s_g[j], (w * (TILES // RING) + i) * 16 + 16)
                        t.matmul(ring_ps[j % 4][:, 0:K * WIN], G[:, j, :],
                                 S[:, j, :, :].rearrange("p k j -> p (k j)"),
                                 start=True, stop=True).then_inc(s_mm, 1)
            pe.wait_ge(s_add, n_pass * TILES + 4)
            for h in range(HB):
                if h >= 4:
                    pe.wait_ge(s_fin, h - 3)
                for k in range(K):
                    last = t.matmul(ring_ps[h % 4][:, 0:D], sums[:, k, h * P:(h + 1) * P], W1[:, k, :],
                                    start=(k == 0), stop=(k == K - 1))
                last.then_inc(s_y, 1)

        @block.vector
        def _(dve):
            v = nc.vector
            chain = [0]

            def done(ins):
                chain[0] += 1
                ins.then_inc(s_dve, 1)
                dve.wait_ge(s_dve, chain[0])

            dve.wait_ge(s_const, 1)
            done(v.tensor_scalar(part_id[:, :], part_id[:, :], R - 1, None, ALU.bitwise_and))
            v.tensor_copy(rel_id[:, :], part_id[:, :])
            dve.wait_ge(s_ldst, 48)
            done(v.tensor_copy(dst_t[:, :, :], dst_ti[:, :, :]))
            done(v.tensor_scalar(rel_t[:, :, :], dst_t[:, :, :], 0.0, 8192.0, ALU.is_lt, ALU.mult))
            done(v.tensor_tensor(rel_t[:, :, :], rel_t[:, :, :], dst_t[:, :, :], ALU.add))
            v.tensor_reduce(max_t[:, :], dst_t[:, :, :], AX_X, ALU.max)
            done(v.tensor_reduce(base_t[:, :], rel_t[:, :, :], AX_X, ALU.min))
            done(v.tensor_scalar(base_t[:, :], base_t[:, :], float(LAST_BASE), None, ALU.min))
            for g in range(TG):
                last = v.tensor_scalar(rel_t[:, g, :], dst_t[:, g, :], base_t[:, g:g + 1], None, ALU.subtract)
            dve.wait_ge(s_lsrc, 48)
            last = v.tensor_copy(src_t[:, :, :], src_ti[:, :, :])
            last.then_inc(s_tab, 1)
            dve.wait_ge(s_tr, 1)
            v.tensor_copy(base_i[:, :], misc[0][0:1, :])
            v.tensor_copy(base_row0[:, :], misc[0][0:1, :])
            done(v.tensor_copy(base_row[:, :], misc[0][0:1, :]))
            done(v.tensor_tensor(span_row[:, :], misc[1][0:1, :], base_row[:, :], ALU.subtract))
            done(v.tensor_reduce(span_max[:, :], span_row[:, :], AX_X, ALU.max))
            done(v.tensor_scalar(win_ends[:, :], win_ends[:, :], span_max[:, :], None, ALU.is_le))
            done(v.tensor_reduce(npass_f[:, :], win_ends[:, :], AX_X, ALU.add))
            done(v.tensor_scalar(npass_f[:, :], npass_f[:, :], 1.0, None, ALU.add))
            v.tensor_copy(npass_i[:, :], npass_f[:, :]).then_inc(s_prep, 1)

            dve.wait_ge(s_tr, 4)
            cols = slice(0, TILES)
            v.tensor_copy(relw[:, :], ring_ps[0][:, cols])
            v.tensor_copy(rel[:, :], ring_ps[0][:, cols])
            v.tensor_copy(src_i[:, :], ring_ps[1][:, cols])
            done(v.tensor_copy(int_a[:, :], ring_ps[2][:, cols]))
            done(v.tensor_scalar(src_hi[:, :].bitcast(I32), int_a[:, :], 7, 31, ALU.logical_shift_right, ALU.bitwise_and))
            done(v.tensor_copy(dst_hi[:, :], src_hi[:, :].bitcast(I32)))
            done(v.tensor_scalar(int_a[:, :], int_a[:, :], 127, None, ALU.bitwise_and))
            done(v.tensor_copy(dst_lo[:, :], int_a[:, :]))
            done(v.tensor_scalar(int_a[:, :], src_i[:, :], 127, None, ALU.bitwise_and))
            done(v.tensor_copy(keylo[:, 1, :], int_a[:, :]))
            done(v.tensor_scalar(int_a[:, :], src_i[:, :], 7, None, ALU.logical_shift_right))
            done(v.tensor_copy(src_hi[:, :], int_a[:, :]))
            dve.wait_ge(s_tr, 5)
            done(v.tensor_copy(ew[:, :], ring_ps[3][:, cols]))
            done(v.tensor_tensor(oh_blk[:, :, :], iota_blk[:, :].unsqueeze(1).to_broadcast([P, TILES, HB]),
                                 dst_hi[:, :].unsqueeze(2).to_broadcast([P, TILES, HB]), ALU.is_equal)
                 )
            dve.sem_inc(s_tab, 1)
            dve.sem_inc(s_hist, 16)
            with dve.Fori(0, TILES // 16) as i:
                for j in range(16):
                    if j == 0:
                        dve.wait_ge(s_histmm, i * 16 + 16)
                    v.tensor_scalar(hist_lo[:, j, :], iota_row[:, :], dst_lo[:, bass.ds(i * 16 + j, 1)], None,
                                    ALU.is_equal).then_inc(s_hist, 1)

            for c in range(CHUNKS):
                dve.wait_ge(s_types, 16 * GROUPS * (c + 1))
                if c >= 1:
                    dve.wait_ge(s_cmm, c)
                v.tensor_scalar(oh_type[:, :], types[:, :], rel_id[:, :], None, ALU.is_equal).then_inc(s_oht, 1)
                dve.wait_ge(s_cmm, c + 1)
                for g in range(GROUPS):
                    t0 = g * GT + c * CT
                    last = v.tensor_tensor(
                        coef[:, t0:t0 + CT, :],
                        misc[0][:, 0:CT * GROUPS * K].rearrange("p (j g k) -> p j g k", g=GROUPS, k=K)[:, :, g, :],
                        ew[:, t0:t0 + CT].unsqueeze(2).to_broadcast([P, CT, K]), ALU.mult)
                last.then_inc(s_cev, 1)

            dve.wait_ge(s_deg, 1)
            done(v.reciprocal(dinv[:, :], dinv[:, :]))
            dve.wait_ge(s_lx, 32)
            v.tensor_tensor(Xs[:, :, :], X[:, :, :], dinv[:, :].unsqueeze(2).to_broadcast([P, HB, D]),
                            ALU.mult).then_inc(s_xs, 1)
            dve.wait_ge(s_act, 1)
            v.tensor_tensor(Y[:, :, :], Xs[:, :, :], Xp[0][:, :, :], ALU.subtract).then_inc(s_xs, 1)
            dve.wait_ge(s_act, 2)
            v.tensor_tensor(Xp[2][:, :, :], Y[:, :, :], Xp[1][:, :, :], ALU.subtract).then_inc(s_xs, 1)

            n_pass = passes(dve)

            def next_windows():
                v.tensor_scalar(relw[:, :], relw[:, :], float(-WIN), None, ALU.add).then_inc(s_ohw, 1)
                v.tensor_scalar(base_row[:, :], base_row[:, :], float(WIN), float(LAST_BASE),
                                ALU.add, ALU.min).then_inc(s_ohw, 1)

            def first_windows():
                done(v.tensor_copy(relw[:, :], rel[:, :]))
                done(v.tensor_copy(base_row[:, :], base_row0[:, :]))

            def one_hots(m, b):
                dve.wait_ge(s_stage0, m + 1)
                dve.wait_ge(s_cnt_mm, (m + 1) * BATCH)
                for j in range(BATCH):
                    q = b * BATCH + j
                    v.tensor_scalar(oh_src[:, q, :], iota_row[:, :], stage0[:, b, 1, j:j + 1], None, ALU.is_equal)
                    v.tensor_scalar(oh_key[:, q, :], iota_keys[:, :], stage0[:, b, 0, j:j + 1], None,
                                    ALU.is_equal).then_inc(s_oh, 1)

            def add_batch(w, i, b):
                m = w * NB + i * 2 + b
                for j in range(BATCH):
                    tile = (i * 2 + b) * BATCH + j
                    at = v.value_load(base_i[0:1, bass.ds(tile, 1)], min_val=0, max_val=LAST_BASE)
                    if j == 0:
                        dve.wait_ge(s_z, m + 3)
                    dve.wait_ge(s_zself, w * TILES + tile + 1)
                    ins = v.tensor_tensor(sum0[:, bass.ds(at, WIN)], sum0[:, bass.ds(at, WIN)],
                                          z_ps[b][:, j * WIN:(j + 1) * WIN], ALU.add)
                    ins.then_inc(s_zself, 1)
                dve.wait_ge(s_zself, w * TILES + (tile + 2))
                dve.sem_inc(s_zadd, 1)

            dve.sem_inc(s_zadd, 2)
            dve.sem_inc(s_zself, 1)
            dve.sem_inc(s_oh, OHS)
            dve.wait_ge(s_xTc, -(-HB // 4))
            with dve.Fori(0, n_pass) as w:
                v.tensor_scalar(valid[:, :], relw[:, :], 0.0, None, ALU.is_ge).then_inc(s_ohw, 1)
                v.scalar_tensor_tensor(keylo[:, 0, :], src_hi[:, :], float(WIN), relw[:, :], ALU.mult,
                                       ALU.add).then_inc(s_ohw, 1)
                dve.wait_ge(s_ohw, w * 6 + 2)
                v.scalar_tensor_tensor(valid[:, :], relw[:, :], float(WIN - 1), valid[:, :], ALU.is_le,
                                       ALU.mult).then_inc(s_ohw, 1)
                dve.wait_ge(s_ohw, w * 6 + 3)
                v.scalar_tensor_tensor(keylo[:, 0, :], keylo[:, 0, :], 1.0, valid[:, :], ALU.add,
                                       ALU.mult).then_inc(s_key, 1)
                one_hots(w * NB, 0)
                one_hots(w * NB + 1, 1)
                with dve.Fori(0, NB // 2 - 1) as i:
                    one_hots(w * NB + i * 2 + 2, 0)
                    add_batch(w, i, 0)
                    one_hots(w * NB + i * 2 + 3, 1)
                    add_batch(w, i, 1)
                add_batch(w, NB // 2 - 1, 0)
                add_batch(w, NB // 2 - 1, 1)
                next_windows()
                dve.wait_ge(s_ohw, w * 6 + 5)
                v.tensor_copy(base_i[:, :], base_row[:, :]).then_inc(s_ohw, 1)
                dve.wait_ge(s_ohw, w * 6 + 6)
                dve.sem_inc(s_turn)

            dve.wait_ge(s_lw, 16 * (6 + GROUPS))
            for h in range(HB):
                dve.wait_ge(s_y, h + 1)
                v.scalar_tensor_tensor(Y[:, h, :], ring_ps[h % 4][:, 0:D], dinv[:, h:h + 1], b0_all[:, :],
                                       ALU.mult, ALU.add).then_inc(s_yev, 1)
            dve.wait_ge(s_y, HB + 1)
            done(v.tensor_scalar(bn_a[:, :], misc[0][:, 0:D], 1.0 / N, None, ALU.mult))
            v.tensor_tensor(Y[:, :, :], Y[:, :, :], bn_a[:, :].unsqueeze(1).to_broadcast([P, HB, D]),
                            ALU.subtract).then_inc(s_bn, 1)
            v.tensor_tensor(X[:, :, :], X[:, :, :], beta_all[:, :].unsqueeze(1).to_broadcast([P, HB, D]), ALU.add)
            dve.wait_ge(s_y, HB + 2)
            dve.sem_inc(s_bn, 1)
            dve.wait_ge(s_act, 2 + -(-HB // 4) + 2)
            done(v.reciprocal(bn_b[:, :], bn_b[:, :]))
            done(v.tensor_tensor(bn_b[:, :], bn_b[:, :], gamma_all[:, :], ALU.mult))
            done(v.tensor_tensor(Y[:, :, :], Y[:, :, :], bn_b[:, :].unsqueeze(1).to_broadcast([P, HB, D]), ALU.mult))
            done(v.tensor_tensor(Y[:, :, :], Y[:, :, :], X[:, :, :], ALU.add))
            for h in range(HB):
                last = v.bn_stats(stats[:, h, :], Y[:, h, :])
            done(last)
            for h in range(HB):
                last = v.bn_aggr(mv[:, h, :], stats[:, h, :])
            last.then_inc(s_bn, 1)
            dve.wait_ge(s_act, 2 + -(-HB // 4) + 3)
            done(v.reciprocal(rstd[:, :], rstd[:, :]))
            for h in range(HB):
                last = v.tensor_scalar(Xs[:, h, :], Y[:, h, :], mv[:, h, 0:1], rstd[:, h:h + 1],
                                       ALU.subtract, ALU.mult)
            last.then_inc(s_x1, 1)

            dve.wait_ge(s_zero, 1)
            first_windows()
            done(v.tensor_copy(base_i[:, :], base_row[:, :]))
            dve.sem_inc(s_add, 4)
            with dve.Fori(0, n_pass) as w:
                v.tensor_tensor(ohw[:, :, :], relw[:, :].unsqueeze(2).to_broadcast([P, TILES, WIN]),
                                iota_win[:, :].unsqueeze(1).to_broadcast([P, TILES, WIN]),
                                ALU.is_equal).then_inc(s_tab, 1)
                dve.wait_ge(s_tab, w + 3)
                dve.sem_inc(s_turn)
                with dve.Fori(0, TILES // RING) as i:
                    for b in range(2):
                        t0 = i * RING + b * HALF
                        dve.wait_ge(s_mm, w * TILES + t0 + HALF)
                        v.tensor_tensor(
                            S[:, b * HALF:(b + 1) * HALF, :, :],
                            ohw[:, bass.ds(t0, HALF), :].unsqueeze(2).to_broadcast([P, HALF, K, WIN]),
                            coef[:, bass.ds(t0, HALF), :].unsqueeze(3).to_broadcast([P, HALF, K, WIN]),
                            ALU.mult).then_inc(s_S, 1)
                    for j in range(RING):
                        tile = i * RING + j
                        at = v.value_load(base_i[0:1, bass.ds(tile, 1)], min_val=0, max_val=LAST_BASE)
                        dve.wait_ge(s_mm, w * TILES + tile + (RING + 1))
                        dve.wait_ge(s_add, w * TILES + tile + 4)
                        v.tensor_tensor(sums[:, :, bass.ds(at, WIN)], sums[:, :, bass.ds(at, WIN)],
                                        ring_ps[j % 4][:, 0:K * WIN].rearrange("p (k j) -> p k j", j=WIN),
                                        ALU.add).then_inc(s_add, 1)
                dve.wait_ge(s_add, (w + 1) * TILES + 4)
                v.tensor_scalar(relw[:, :], relw[:, :], float(-WIN), None, ALU.add).then_inc(s_key, 1)
                v.tensor_scalar(base_row[:, :], base_row[:, :], float(WIN), float(LAST_BASE),
                                ALU.add, ALU.min).then_inc(s_key, 1)
                dve.wait_ge(s_key, n_pass + w * 3 + 2)
                v.tensor_copy(base_i[:, :], base_row[:, :]).then_inc(s_key, 1)
                dve.wait_ge(s_key, n_pass + w * 3 + 3)
                dve.sem_inc(s_turn)

            for h in range(HB):
                dve.wait_ge(s_y, HB + 2 + h + 1)
                ins = v.tensor_tensor(Y[:, h, :], ring_ps[h % 4][:, 0:D], b1_all[:, :], ALU.add)
                ins.then_inc(s_fin, 1)
                dve.wait_ge(s_fin, h + 1)
                done(v.scalar_tensor_tensor(Y[:, h, :], Y[:, h, :], 0.0, Xs[:, h, :], ALU.max, ALU.add))
                done(v.bn_stats(stats[:, h, :], Y[:, h, :]))
                v.bn_aggr(mv[:, h, :], stats[:, h, :]).then_inc(s_fev, 1)
                dve.wait_ge(s_fev, h + 1)
                dve.wait_ge(s_act, 2 + -(-HB // 4) + 3 + h + 1)
                done(v.reciprocal(rstd[:, h:h + 1], rstd[:, h:h + 1]))
                v.tensor_scalar(Y[:, h, :], Y[:, h, :], mv[:, h, 0:1], rstd[:, h:h + 1],
                                ALU.subtract, ALU.mult).then_inc(s_outr, 1)


_INS = ['x', 'src', 'dst', 'edge_type_32', 'edge_weight1', 'L0_gnn_W', 'L0_gnn_b', 'L0_gnn_gamma',
        'L0_gnn_beta', 'L1_gnn_weight', 'L1_gnn_w_comp', 'L1_gnn_bias_param']
_OUTS = [((3125, 128), 'float32')]


def kernel(**inputs):
    import numpy as _np
    import concourse.bacc as _bacc
    from concourse import mybir as _mybir
    from concourse.bass_utils import run_bass_kernel_spmd as _run

    nc = _bacc.Bacc("TRN2", target_bir_lowering=False, num_devices=1)
    arrays, args = {}, []
    for name in _INS:
        a = _np.ascontiguousarray(inputs[name])
        arrays[f"in_{name}_dram"] = a
        args.append(nc.dram_tensor(f"in_{name}_dram", a.shape, _mybir.dt.from_np(a.dtype), kind="ExternalInput").ap())
    for i, (shape, dtype) in enumerate(_OUTS):
        dt = _mybir.dt.from_np(_np.dtype(dtype))
        args.append(nc.dram_tensor(f"out_{i}_dram", shape, dt, kind="ExternalOutput").ap())
    args.append(nc.dram_tensor("x1_dram", _OUTS[0][0], _mybir.dt.float32, kind="Internal").ap())
    gnn_kernel(nc, *args)
    r = _run(nc, [arrays], core_ids=[0])
    got = tuple(r.results[0][f"out_{i}_dram"] for i in range(len(_OUTS)))
    return got[0]
```

```python
from contextlib import ExitStack

import concourse.bass as bass
import numpy as np
from concourse import mybir

F32 = mybir.dt.float32
BF16 = mybir.dt.bfloat16
FP16 = mybir.dt.float16
I32 = mybir.dt.int32
ALU = mybir.AluOpType
ACT = mybir.ActivationFunctionType
AX_X = mybir.AxisListType.X

P = 128
EPS = 1e-5


def gnn_kernel(nc, x, src, dst, etype, eweight, w0, b0, gamma, beta, w1, wcomp, b1, out, x1_dram):
    N, D = x.shape
    E = src.shape[0]
    K = w1.shape[0]
    R = wcomp.shape[0]
    assert D == P
    TILES = -(-E // P)
    UNIT = 32
    TILES = -(-TILES // UNIT) * UNIT
    HB = -(-N // P)
    NTAIL = N - (HB - 1) * P
    NPAD = HB * P
    WIN = 12
    LAST_BASE = NPAD - WIN
    PASSES = -(-N // WIN) + 1
    KEYS = HB * WIN
    BATCH = 16
    NB = TILES // BATCH
    BW = BATCH * WIN
    TG = -(-TILES // P)
    TLAST = TILES - (TG - 1) * P
    FULL_ROWS = E // P - (TG - 1) * P
    REST = E % P
    HALF = 8
    RING = 2 * HALF
    QUAD = 4
    NQ = RING // QUAD
    GROUPS = P // R
    GT = TILES // GROUPS
    CT = 8
    CHUNKS = GT // CT
    CW = CT * GROUPS * K
    TYPE_SLOTS = 3
    assert GT % CT == 0 and CW <= 512 and TLAST == 32 and 0 < REST

    with ExitStack() as ctx:
        def sb(name, shape, dt):
            return ctx.enter_context(nc.sbuf_tensor(name, shape, dt))

        def ps(name, shape, dt=F32):
            return ctx.enter_context(nc.psum_tensor(name, shape, dt))

        def sem(name):
            return ctx.enter_context(nc.semaphore(name))

        ident = sb("ident", [P, P], F32)
        ones = sb("ones", [P, P], F32)
        iota_row = sb("iota_row", [P, P], FP16)
        iota_keys = sb("iota_keys", [P, KEYS], FP16)
        iota_blk = sb("iota_blk", [P, HB], F32)
        iota_win = sb("iota_win", [P, WIN], F32)
        win_ends = sb("win_ends", [1, PASSES], F32)
        part_id = sb("part_id", [P, 1], I32)
        rel_id = sb("rel_id", [P, 1], F32)
        X = sb("X", [P, HB, D], F32)
        W0 = sb("W0", [P, D], F32)
        W1 = sb("W1", [P, K, D], F32)
        b0_all = sb("b0_all", [P, D], F32)
        gamma_all = sb("gamma_all", [P, D], F32)
        beta_all = sb("beta_all", [P, D], F32)
        b1_col = sb("b1_col", [P, 1], F32)
        wblk = sb("wblk", [P, GROUPS, K], F32)
        ew_t = sb("ew_t", [P, TG, P], F32)
        base_t = sb("base_t", [P, TG], F32)
        max_t = sb("max_t", [P, TG], F32)
        rel = sb("rel", [P, TILES], F32)
        relw = sb("relw", [P, TILES], F32)
        ew = sb("ew", [P, TILES], F32)
        src_i = sb("src_i", [P, TILES + RING], I32)
        ohw = sb("ohw", [P, TILES, WIN], BF16)
        zeros = sb("zeros", [P, P], BF16)
        base_row0 = sb("base_row0", [1, TG * P], F32)
        coef = sb("coef", [P, TILES, K], F32)
        base_row = sb("base_row", [1, TG * P], F32)
        span_row = sb("span_row", [1, TG * P], F32)
        base_i = sb("base_i", [1, TG * P], I32)
        span_max = sb("span_max", [1, 1], F32)
        npass_f = sb("npass_f", [1, 1], F32)
        npass_i = sb("npass_i", [1, 1], I32)
        dinv = sb("dinv", [P, HB], F32)
        Xs_all = sb("Xs", [P, HB * D], F32)
        Xs = Xs_all[:, :].rearrange("p (h f) -> p h f", h=HB)
        OHS = 2 * BATCH
        stage0 = sb("stage0", [P, 2, 2, BATCH], F32)
        sum0 = sb("sum0", [P, NPAD], F32)
        sum1 = sb("sum1", [P, NPAD], F32)

        def inside(space, at, dt, *dims):
            words = -(-int(np.prod(dims)) * (4 if dt in (F32, I32) else 2) // 4)
            assert at + words <= space.shape[1]
            names = "abcd"[:len(dims)]
            view = space[:, at:at + words].bitcast(dt).rearrange(
                f"p ({' '.join(names)}) -> p {' '.join(names)}", **dict(zip(names, dims)))
            return view, at + words

        Xp = [sb(f"Xp{i}", [P, HB, D], BF16) for i in range(3)]
        oh_src = sb("oh_src", [P, OHS, P], BF16)
        oh_key = sb("oh_key", [P, OHS, KEYS], BF16)
        HS = 16
        ITEMS = TG * WIN
        hist_lo = sb("hist_lo", [P, HS, P], BF16)
        Y_all = sb("Y", [P, HB * D], F32)
        Y = Y_all[:, :].rearrange("p (h f) -> p h f", h=HB)
        hist_blk, at = inside(Y_all, 0, BF16, ITEMS, HB)
        is_node, at = inside(Y_all, at, BF16, 2, WIN, P)
        room = sb("room", [P, (TYPE_SLOTS + 2) * CT * P], F32)
        types, at = inside(room, 0, I32, TYPE_SLOTS, CT * P)
        oh_type, at = inside(room, at, F32, 2, CT * P)
        counts, at = inside(room, 0, BF16, 2, HB, BW)
        dst_ti, at = inside(Xs_all, 0, I32, TG, P)
        src_ti, at = inside(Xs_all, at, I32, TG, P)
        dst_t, at = inside(Xs_all, at, F32, TG, P)
        src_t, at = inside(Xs_all, at, F32, TG, P)
        rel_t, at = inside(Xs_all, at, F32, TG, P)
        idx = sb("idx", [P, 2, HALF], I32)
        rings = sb("rings", [P, RING * D + RING * K * WIN], F32)
        G, at = inside(rings, 0, F32, RING, D)
        S, at = inside(rings, at, F32, RING, K, WIN)
        keylo, at = inside(rings, 0, F32, 2, TILES)
        src_hi, at = inside(rings, at, F32, TILES)
        valid, at = inside(rings, at, F32, TILES)
        int_a, at = inside(rings, at, I32, TILES)
        node_cnt, at = inside(rings, at, F32, ITEMS)
        node_i, at = inside(rings, at, I32, ITEMS)
        node_bits, at = inside(rings, at, I32, ITEMS)
        node_lo, at = inside(rings, at, F32, ITEMS)
        node_hi, at = inside(rings, at, F32, ITEMS)
        by_basis = sb("by_basis", [P, K, RING * WIN], F32)
        stats = sb("stats", [P, HB, 6], F32)
        mv = sb("mv", [P, HB, 2], F32)
        rstd = sb("rstd", [P, HB], F32)
        bn_a = sb("bn_a", [P, D], F32)
        bn_b = sb("bn_b", [P, D], F32)
        eps_c = sb("eps_c", [P, 1], F32)

        ring_ps = [ps(f"ring_ps{i}", [P, 512]) for i in range(4)]
        z_ps = [ps(f"z_ps{i}", [P, 512]) for i in range(2)]
        misc = [ps(f"misc{i}", [P, 512]) for i in range(2)]
        coef_ps = [z_ps[0], ring_ps[3]]

        s_iota = sem("s_iota")
        s_const = sem("s_const")
        s_pad = sem("s_pad")
        s_ldst = sem("s_ldst")
        s_lsrc = sem("s_lsrc")
        s_lew = sem("s_lew")
        s_lx = sem("s_lx")
        s_lw = sem("s_lw")
        s_types = [sem(f"s_types{i}") for i in range(TYPE_SLOTS)]
        s_dve = sem("s_dve")
        s_loop = sem("s_loop")
        s_tr = sem("s_tr")
        s_tab = sem("s_tab")
        s_prep = sem("s_prep")
        s_hist = sem("s_hist")
        s_histmm = sem("s_histmm")
        s_oht = sem("s_oht")
        s_cmm = sem("s_cmm")
        s_cev = sem("s_cev")
        s_deg = sem("s_deg")
        s_act = sem("s_act")
        s_xs = sem("s_xs")
        s_xT = sem("s_xT")
        s_xTc = sem("s_xTc")
        s_key = sem("s_key")
        s_stage0 = sem("s_stage0")
        s_oh = sem("s_oh")
        s_cnt_mm = sem("s_cnt_mm")
        s_cnt = sem("s_cnt")
        s_z = sem("s_z")
        s_zadd = sem("s_zadd")
        s_turn = sem("s_turn")
        s_y = sem("s_y")
        s_yev = sem("s_yev")
        s_bn = sem("s_bn")
        s_x1 = sem("s_x1")
        s_x1st = sem("s_x1st")
        s_stage1 = sem("s_stage1")
        s_g = [sem(f"s_g{i}") for i in range(RING)]
        s_S = sem("s_S")
        s_mm = sem("s_mm")
        s_add = sem("s_add")
        s_fin = sem("s_fin")
        s_fev = sem("s_fev")
        s_outr = sem("s_outr")
        s_out = sem("s_out")
        s_ohw = sem("s_ohw")
        s_relid = sem("s_relid")
        s_ew = sem("s_ew")
        s_coef = sem("s_coef")
        s_quad = sem("s_quad")
        s_byb = sem("s_byb")
        s_r = sem("s_r")
        s_tfin = sem("s_tfin")

        def passes(eng):
            eng.wait_ge(s_prep, 1)
            return eng.value_load(npass_i[0:1, 0:1], min_val=1, max_val=PASSES)

        def block_rows(h):
            return P if h < HB - 1 else NTAIL

        def edges_by_tile(a):
            full = (TG - 1) * P * P
            return (a[0:full].rearrange("(g t p) -> t g p", t=P, p=P),
                    a[full:full + FULL_ROWS * P].rearrange("(t p) -> t p", p=P),
                    a[full + FULL_ROWS * P:E].rearrange("(t p) -> t p", t=1))

        block = ctx.enter_context(nc.Block())

        @block.sync
        def _(sp):
            def load_edges(tile, a, signal):
                main, rows, rest = edges_by_tile(a)
                sp.dma_start(tile[:, 0:TG - 1, :], main).then_inc(signal, 16)
                sp.dma_start(tile[0:FULL_ROWS, TG - 1, :], rows).then_inc(signal, 16)
                sp.dma_start(tile[FULL_ROWS:FULL_ROWS + 1, TG - 1, 0:REST], rest).then_inc(signal, 16)

            sp.wait_ge(s_pad, 1)
            load_edges(dst_ti, dst, s_ldst)
            load_edges(src_ti, src, s_lsrc)
            load_edges(ew_t, eweight.rearrange("e o -> (e o)"), s_lew)
            sp.wait_ge(s_pad, 2)
            for c in range(CHUNKS):
                if c >= TYPE_SLOTS:
                    sp.wait_ge(s_oht, c - TYPE_SLOTS + 1)
                for g in range(GROUPS):
                    e0 = (g * GT + c * CT) * P
                    n = min(CT * P, E - e0)
                    sp.dma_start(types[g * R:(g + 1) * R, c % TYPE_SLOTS, 0:n],
                                 etype[e0:e0 + n].partition_broadcast(R)).then_inc(s_types[c % TYPE_SLOTS], 16)
            sp.wait_ge(s_x1, 1)
            sp.dma_start(x1_dram[0:(HB - 1) * P, :].rearrange("(h p) f -> p h f", p=P),
                         Xs[:, 0:HB - 1, :]).then_inc(s_x1st, 16)
            sp.dma_start(x1_dram[(HB - 1) * P:N, :], Xs[0:NTAIL, HB - 1, :]).then_inc(s_x1st, 16)
            for h in range(HB):
                sp.wait_ge(s_outr, h + 1)
                n = block_rows(h)
                sp.dma_start(out[h * P:h * P + n, :], Y[0:n, h, :]).then_inc(s_out, 16)
            sp.wait_ge(s_out, 16 * HB)

        @block.gpsimd
        def _(pool):
            g = nc.gpsimd
            g.memset(dst_ti[:, TG - 1, :], -1)
            g.memset(src_ti[:, TG - 1, :], 0)
            g.memset(ew_t[:, TG - 1, :], 0.0).then_inc(s_pad, 1)
            g.memset(types[:, :, :], 0).then_inc(s_pad, 1)
            g.memset(X[:, HB - 1, :], 0.0)
            g.memset(wblk[:, :, :], 0.0).then_inc(s_pad, 1)
            g.memset(ones[:, :], 1.0)
            g.memset(zeros[:, :], 0.0)
            g.memset(ident[:, :], 0.0).then_inc(s_iota, 1)
            pool.wait_ge(s_iota, 1)
            g.affine_select(out=ident[:, :], in_=ident[:, :], compare_op=ALU.not_equal, fill=1.0, base=0,
                            pattern=[[-1, P]], channel_multiplier=1)
            g.memset(eps_c[:, :], EPS)
            imprecise = dict(allow_small_or_imprecise_dtypes=True)
            g.iota(iota_row[:, :], [[1, P]], base=0, channel_multiplier=0, **imprecise)
            g.iota(iota_keys[:, :], [[1, KEYS]], base=1, channel_multiplier=0, **imprecise)
            g.iota(iota_blk[:, :], [[1, HB]], base=0, channel_multiplier=0, **imprecise)
            g.iota(iota_win[:, :], [[1, WIN]], base=0, channel_multiplier=0, **imprecise)
            g.iota(win_ends[:, :], [[WIN, PASSES]], base=WIN, channel_multiplier=0, **imprecise)
            g.iota(part_id[:, :], [[0, 1]], base=0, channel_multiplier=1).then_inc(s_const, 1)

            pool.wait_ge(s_relid, 1)
            for c in range(CHUNKS):
                pool.wait_ge(s_types[c % TYPE_SLOTS], 16 * GROUPS * (c // TYPE_SLOTS + 1))
                if c >= 2:
                    pool.wait_ge(s_cmm, c - 1)
                g.tensor_scalar(oh_type[:, c % 2, :], types[:, c % TYPE_SLOTS, :], rel_id[:, :], None,
                                ALU.is_equal).then_inc(s_oht, 1)

            pool.wait_ge(s_cev, CHUNKS)
            pool.wait_ge(s_ew, 1)
            g.tensor_tensor(coef[:, :, :], coef[:, :, :], ew[:, :].unsqueeze(2).to_broadcast([P, TILES, K]),
                            ALU.mult).then_inc(s_coef, 1)

            n_pass = passes(pool)
            with pool.Fori(0, n_pass) as w:
                pool.wait_ge(s_key, w + 1)
                pool.sem_inc(s_turn)
                with pool.Fori(0, NB // 2) as i:
                    for b in range(2):
                        m = w * NB + i * 2 + b
                        pool.wait_ge(s_oh, (m + 1) * BATCH)
                        g.tensor_copy(stage0[:, b, :, :],
                                      keylo[:, :, bass.ds((i * 2 + b) * BATCH, BATCH)]).then_inc(s_stage0, 1)

            pool.wait_ge(s_x1st, 32)
            with pool.Fori(0, n_pass) as w:
                with pool.Fori(0, TILES // RING) as i:
                    for b in range(2):
                        pool.wait_ge(s_stage1, w * (TILES // HALF) + i * 2 + b + 1)
                        pool.sem_inc(s_turn)
                        for j in range(HALF):
                            q = b * HALF + j
                            g.indirect_dma_start(G[:, q, :], None, x1_dram[:, :],
                                                 bass.IndirectOffsetOnAxis(ap=idx[:, b, j:j + 1], axis=0)
                                                 ).then_inc(s_g[q], 16)

        @block.scalar
        def _(act):
            a = nc.scalar
            act.dma_start(X[:, 0:HB - 1, :],
                          x[0:(HB - 1) * P, :].rearrange("(h p) f -> p h f", p=P)).then_inc(s_lx, 16)
            act.dma_start(W0[:, :], w0).then_inc(s_lw, 16)
            act.dma_start(W1[:, :, :], w1.rearrange("k f o -> f k o")).then_inc(s_lw, 16)
            for vec, tile in ((b0, b0_all), (gamma, gamma_all), (beta, beta_all)):
                act.dma_start(tile[:, :], vec.partition_broadcast(P)).then_inc(s_lw, 16)
            with nc.allow_non_contiguous_dma("one vector, once"):
                act.dma_start(b1_col[:, :], b1.rearrange("(o u) -> o u", u=1)).then_inc(s_lw, 16)
            act.wait_ge(s_pad, 3)
            act.dma_start(X[0:NTAIL, HB - 1, :], x[(HB - 1) * P:N, :]).then_inc(s_lx, 16)
            for g in range(GROUPS):
                act.dma_start(wblk[g * R:(g + 1) * R, g, :], wcomp).then_inc(s_lw, 16)

            for c in range(CHUNKS):
                act.wait_ge(s_cmm, c + 1)
                part = slice(c * CT, (c + 1) * CT)
                a.copy(coef[:, :, :].rearrange("p (g t) k -> p g t k", g=GROUPS)[:, :, part, :],
                       coef_ps[c % 2][:, 0:CW].rearrange("p (t g k) -> p g t k", g=GROUPS, k=K)
                       ).then_inc(s_cev, 1)
            n_pass = passes(act)
            act.wait_ge(s_histmm, n_pass * ITEMS + HS)
            a.activation(dinv[:, :], misc[1][:, 0:HB], ACT.Sqrt, bias=ones[:, 0:1]).then_inc(s_deg, 1)
            act.wait_ge(s_xs, 1)
            a.copy(Xp[0][:, :, :], Xs[:, :, :]).then_inc(s_act, 1)
            act.wait_ge(s_xs, 2)
            a.copy(Xp[1][:, :, :], Y[:, :, :]).then_inc(s_act, 1)
            for q in range(-(-HB // 4)):
                n = min(4, HB - 4 * q)
                act.wait_ge(s_xT, q + 1)
                a.copy(sum0[:, 4 * q * P:(4 * q + n) * P], z_ps[q % 2][:, 0:n * P]).then_inc(s_xTc, 1)

            act.sem_inc(s_cnt, 4)
            with act.Fori(0, n_pass) as w:
                with act.Fori(0, NB // 2) as i:
                    for b in range(2):
                        m = w * NB + i * 2 + b
                        act.wait_ge(s_z, m + 1)
                        for j in range(BATCH):
                            act.wait_ge(s_cnt_mm, m * BATCH + (OHS + j + 1))
                            a.copy(counts[:, b, :, j * WIN:(j + 1) * WIN],
                                   ring_ps[j % 4][:, 0:KEYS].rearrange("p (h j) -> p h j", j=WIN)
                                   ).then_inc(s_cnt, 1)

            for q in range(-(-HB // 4)):
                n = min(4, HB - 4 * q)
                act.wait_ge(s_yev, 4 * q + n)
                a.activation(Y[:, 4 * q:4 * q + n, :], Y[:, 4 * q:4 * q + n, :], ACT.Relu).then_inc(s_act, 1)
            n_act = 2 + -(-HB // 4)
            act.wait_ge(s_bn, 1)
            a.activation(Xs[:, :, :], Y[:, :, :], ACT.Square).then_inc(s_act, 1)
            act.wait_ge(s_bn, 2)
            a.activation(bn_b[:, :], misc[1][:, 0:D], ACT.Sqrt, bias=eps_c[:, :], scale=1.0 / N).then_inc(s_act, 1)
            act.wait_ge(s_bn, 3)
            a.activation(rstd[:, :], mv[:, :, 1], ACT.Sqrt, bias=eps_c[:, :]).then_inc(s_act, 1)

            act.wait_ge(s_y, HB)
            a.activation(sum1[:, :], sum0[:, :], ACT.Identity, bias=b1_col[:, :], scale=0.0).then_inc(s_act, 1)

            act.sem_inc(s_byb, NQ)
            for b in range(2):
                a.copy(idx[:, b, :], src_i[:, b * HALF:(b + 1) * HALF]).then_inc(s_stage1, 1)
            with act.Fori(0, n_pass) as w:
                with act.Fori(0, TILES // RING) as i:
                    for q in range(NQ):
                        act.wait_ge(s_mm, w * TILES + i * RING + (RING + (q + 1) * QUAD))
                        if q == 0:
                            act.wait_ge(s_r, w * (TILES // RING) + i + 1)
                        a.copy(by_basis[:, :, q * QUAD * WIN:(q + 1) * QUAD * WIN].rearrange("p k (t j) -> p t k j", t=QUAD),
                               ring_ps[q][:, 0:QUAD * K * WIN].rearrange("p (t k j) -> p t k j", t=QUAD, k=K)
                               ).then_inc(s_byb, 1)
                        if q % 2 == 1:
                            t0 = i * RING + (RING + (q // 2) * HALF)
                            a.copy(idx[:, q // 2, :], src_i[:, bass.ds(t0, HALF)]).then_inc(s_stage1, 1)
            for q in range(-(-HB // 4)):
                act.wait_ge(s_fev, q + 1)
                hs = slice(4 * q, min(4 * q + 4, HB))
                a.activation(rstd[:, hs], mv[:, hs, 1], ACT.Sqrt, bias=eps_c[:, :]).then_inc(s_act, 1)

        @block.tensor
        def _(pe):
            t = nc.tensor
            pe.wait_ge(s_const, 1)
            pe.wait_ge(s_tab, 1)
            for k, col in ((0, base_t), (1, max_t)):
                for g in range(TG):
                    last = t.matmul(misc[k][0:1, g * P:(g + 1) * P], col[:, g:g + 1], ident[:, :],
                                    start=True, stop=True)
            last.then_inc(s_tr, 1)
            pe.wait_ge(s_lew, 48)
            for k, by_tile in enumerate((rel_t, src_t, ew_t)):
                for g in range(TG):
                    n = P if g < TG - 1 else TLAST
                    last = t.transpose(ring_ps[k][:, g * P:g * P + n], by_tile[0:n, g, :], ident[0:n, 0:n])
                last.then_inc(s_tr, 1)
            pe.wait_ge(s_lw, 16 * (6 + GROUPS))
            for c in range(CHUNKS):
                pe.wait_ge(s_oht, c + 1)
                if c >= 2:
                    pe.wait_ge(s_cev, c - 1)
                for j in range(CT):
                    last = t.matmul(coef_ps[c % 2][:, j * GROUPS * K:(j + 1) * GROUPS * K],
                                    oh_type[:, c % 2, j * P:(j + 1) * P], wblk[:, :, :].rearrange("p g k -> p (g k)"),
                                    start=True, stop=True)
                last.then_inc(s_cmm, 1)
            n_pass = passes(pe)
            t.matmul(misc[1][:, 0:HB], zeros[:, :], zeros[:, 0:HB], start=True, stop=False,
                     skip_group_check=True)
            pe.sem_inc(s_histmm, HS)
            with pe.Fori(0, n_pass) as w:
                for q in range(ITEMS):
                    pe.wait_ge(s_hist, w * ITEMS + (q + 1))
                    t.matmul(misc[1][:, 0:HB], hist_lo[:, q % HS, :], hist_blk[:, q, :],
                             start=False, stop=False, skip_group_check=True).then_inc(s_histmm, 1)
            pe.wait_ge(s_cev, CHUNKS)
            pe.wait_ge(s_xs, 1)
            for q in range(-(-HB // 4)):
                if q >= 2:
                    pe.wait_ge(s_xTc, q - 1)
                for j in range(min(4, HB - 4 * q)):
                    last = t.transpose(z_ps[q % 2][:, j * P:(j + 1) * P], Xs[:, 4 * q + j, :], ident[:, :])
                last.then_inc(s_xT, 1)
            pe.wait_ge(s_xTc, -(-HB // 4))

            pe.sem_inc(s_cnt_mm, OHS)
            pe.sem_inc(s_z, 2)
            pe.sem_inc(s_mm, RING)

            def count(m, b, j):
                if j % 4 == 0:
                    pe.wait_ge(s_oh, m * BATCH + (OHS + j + 4))
                if j % 2 == 0:
                    pe.wait_ge(s_cnt, m * BATCH + (j + 2))
                t.matmul(ring_ps[j % 4][:, 0:KEYS], oh_src[:, b * BATCH + j, :],
                         oh_key[:, b * BATCH + j, :], start=True, stop=True).then_inc(s_cnt_mm, 1)

            def aggregate(m, b, j):
                if j == 0:
                    pe.wait_ge(s_cnt, m * BATCH + (4 + BATCH))
                    pe.wait_ge(s_zadd, m + 1)
                for q in range(j * 3 * HB // BATCH, (j + 1) * 3 * HB // BATCH):
                    last = t.matmul(z_ps[b][:, 0:BW], Xp[q % 3][:, q // 3, :], counts[:, b, q // 3, :],
                                    start=(q == 0), stop=(q == 3 * HB - 1))
                if j == BATCH - 1:
                    last.then_inc(s_z, 1)

            def step(m, b):
                count(m + 1, 1 - b, 0)
                count(m + 1, 1 - b, 1)
                for j in range(BATCH):
                    aggregate(m, b, j)
                    if j + 2 < BATCH:
                        count(m + 1, 1 - b, j + 2)

            pe.wait_ge(s_cev, CHUNKS)
            pe.wait_ge(s_ew, 1)
            pe.wait_ge(s_act, 2)
            pe.wait_ge(s_xs, 3)
            with pe.Fori(0, n_pass) as w:
                for j in range(BATCH):
                    count(w * NB, 0, j)
                with pe.Fori(0, NB // 2 - 1) as i:
                    step(w * NB + i * 2, 0)
                    step(w * NB + i * 2 + 1, 1)
                step(w * NB + NB - 2, 0)
                for j in range(BATCH):
                    aggregate(w * NB + NB - 1, 1, j)

            pe.wait_ge(s_zadd, n_pass * NB + 2)
            for h in range(HB):
                if h >= 4:
                    pe.wait_ge(s_yev, h - 3)
                t.matmul(ring_ps[h % 4][:, 0:D], sum0[:, h * P:(h + 1) * P], W0[:, :],
                         start=True, stop=True).then_inc(s_y, 1)
            for k in range(2):
                vals = Y if k == 0 else Xs
                if k == 1:
                    pe.wait_ge(s_act, 2 + -(-HB // 4) + 1)
                for h in range(HB):
                    if k == 0:
                        pe.wait_ge(s_act, 2 + h // 4 + 1)
                    n = block_rows(h)
                    last = t.matmul(misc[k][:, 0:D], ones[0:n, :], vals[0:n, h, :], start=(h == 0), stop=(h == HB - 1))
                last.then_inc(s_y, 1)

            pe.sem_inc(s_r, 1)
            with pe.Fori(0, n_pass) as w:
                with pe.Fori(0, TILES // RING) as i:
                    ring = w * (TILES // RING) + i
                    for q in range(NQ):
                        if q % 2 == 0:
                            pe.wait_ge(s_S, ring * 2 + (q // 2 + 1))
                        pe.wait_ge(s_byb, ring * NQ + (q + 1))
                        for j in range(q * QUAD, (q + 1) * QUAD):
                            pe.wait_ge(s_g[j], ring * 16 + 16)
                            at = (j - q * QUAD) * K * WIN
                            t.matmul(ring_ps[q][:, at:at + K * WIN], G[:, j, :],
                                     S[:, j, :, :].rearrange("p k j -> p (k j)"),
                                     start=True, stop=True).then_inc(s_mm, 1)
                    pe.wait_ge(s_byb, ring * NQ + 2 * NQ)
                    pe.wait_ge(s_add, ring + 1)
                    for k in range(K):
                        last = t.matmul(z_ps[0][:, 0:RING * WIN], W1[:, k, :], by_basis[:, k, :],
                                        start=(k == 0), stop=(k == K - 1))
                    last.then_inc(s_r, 1)
            pe.wait_ge(s_add, n_pass * (TILES // RING) + 1)
            for h in range(HB):
                if h >= 4:
                    pe.wait_ge(s_fin, h - 3)
                t.transpose(ring_ps[h % 4][:, 0:P], sum1[:, h * P:(h + 1) * P], ident[:, :]).then_inc(s_tfin, 1)

        @block.vector
        def _(dve):
            v = nc.vector
            class Chain:

                def __init__(self, counter):
                    self.counter, self.n = counter, 0

                def restart(self):
                    dve.sem_inc(s_turn)
                    dve.sem_clear(self.counter)
                    self.n = 0

                def done(self, ins):
                    self.n += 1
                    ins.then_inc(self.counter, 1)
                    dve.wait_ge(self.counter, self.n)

            done = Chain(s_dve).done
            loop = Chain(s_loop)

            dve.wait_ge(s_const, 1)
            done(v.tensor_scalar(part_id[:, :], part_id[:, :], R - 1, None, ALU.bitwise_and))
            v.tensor_copy(rel_id[:, :], part_id[:, :]).then_inc(s_relid, 1)
            dve.wait_ge(s_ldst, 48)
            done(v.tensor_copy(dst_t[:, :, :], dst_ti[:, :, :]))
            done(v.tensor_scalar(rel_t[:, :, :], dst_t[:, :, :], 0.0, 8192.0, ALU.is_lt, ALU.mult))
            done(v.tensor_tensor(rel_t[:, :, :], rel_t[:, :, :], dst_t[:, :, :], ALU.add))
            v.tensor_reduce(max_t[:, :], dst_t[:, :, :], AX_X, ALU.max)
            done(v.tensor_reduce(base_t[:, :], rel_t[:, :, :], AX_X, ALU.min))
            done(v.tensor_scalar(base_t[:, :], base_t[:, :], float(LAST_BASE), None, ALU.min))
            for g in range(TG):
                last = v.tensor_scalar(rel_t[:, g, :], dst_t[:, g, :], base_t[:, g:g + 1], None, ALU.subtract)
            dve.wait_ge(s_lsrc, 48)
            last = v.tensor_copy(src_t[:, :, :], src_ti[:, :, :])
            last.then_inc(s_tab, 1)
            dve.wait_ge(s_tr, 1)
            v.tensor_copy(base_i[:, :], misc[0][0:1, :])
            v.tensor_copy(base_row0[:, :], misc[0][0:1, :])
            done(v.tensor_copy(base_row[:, :], misc[0][0:1, :]))
            done(v.tensor_tensor(span_row[:, :], misc[1][0:1, :], base_row[:, :], ALU.subtract))
            done(v.tensor_reduce(span_max[:, :], span_row[:, :], AX_X, ALU.max))
            done(v.tensor_scalar(win_ends[:, :], win_ends[:, :], span_max[:, :], None, ALU.is_le))
            done(v.tensor_reduce(npass_f[:, :], win_ends[:, :], AX_X, ALU.add))
            done(v.tensor_scalar(npass_f[:, :], npass_f[:, :], 1.0, None, ALU.add))
            v.tensor_copy(npass_i[:, :], npass_f[:, :]).then_inc(s_prep, 1)

            n_pass = passes(dve)
            dve.wait_ge(s_tr, 2)
            item = [P, TG, WIN]
            with dve.Fori(0, n_pass) as w:
                loop.restart()
                for g in range(TG):
                    eq = is_node[:, g % 2, :, :]
                    loop.done(v.tensor_tensor(eq, rel_t[:, g, :].unsqueeze(1).to_broadcast([P, WIN, P]),
                                              iota_win[:, :].unsqueeze(2).to_broadcast([P, WIN, P]), ALU.is_equal))
                    last = v.tensor_reduce(node_cnt[:, g * WIN:(g + 1) * WIN], eq, AX_X, ALU.add)
                loop.done(last)
                loop.done(v.tensor_tensor(node_i[:, :].rearrange("p (g j) -> p g j", g=TG),
                                          base_t[:, :].unsqueeze(2).to_broadcast(item),
                                          iota_win[:, :].unsqueeze(1).to_broadcast(item), ALU.add))
                loop.done(v.tensor_scalar(node_bits[:, :], node_i[:, :], 127, None, ALU.bitwise_and))
                loop.done(v.tensor_copy(node_lo[:, :], node_bits[:, :]))
                loop.done(v.tensor_scalar(node_bits[:, :], node_i[:, :], 7, None, ALU.logical_shift_right))
                loop.done(v.tensor_copy(node_hi[:, :], node_bits[:, :]))
                dve.wait_ge(s_histmm, w * ITEMS + HS)
                loop.done(v.tensor_tensor(hist_blk[:, :, :], node_hi[:, :].unsqueeze(2).to_broadcast([P, ITEMS, HB]),
                                          iota_blk[:, :].unsqueeze(1).to_broadcast([P, ITEMS, HB]), ALU.is_equal))
                for q in range(ITEMS):
                    if q % HS == 0 and q:
                        dve.wait_ge(s_histmm, w * ITEMS + (q + HS))
                    v.tensor_scalar(hist_lo[:, q % HS, :], iota_row[:, :], node_lo[:, q:q + 1],
                                    node_cnt[:, q:q + 1], ALU.is_equal, ALU.mult).then_inc(s_hist, 1)
                v.tensor_scalar(rel_t[:, :, :], rel_t[:, :, :], float(-WIN), None, ALU.add)
                loop.done(v.tensor_scalar(base_t[:, :], base_t[:, :], float(WIN), float(LAST_BASE), ALU.add, ALU.min))

            dve.wait_ge(s_tr, 3)
            cols = slice(0, TILES)
            v.tensor_copy(relw[:, :], ring_ps[0][:, cols])
            v.tensor_copy(rel[:, :], ring_ps[0][:, cols])
            v.tensor_copy(src_i[:, TILES:TILES + RING], ring_ps[1][:, 0:RING])
            done(v.tensor_copy(src_i[:, cols], ring_ps[1][:, cols]))
            done(v.tensor_scalar(int_a[:, :], src_i[:, cols], 127, None, ALU.bitwise_and))
            done(v.tensor_copy(keylo[:, 1, :], int_a[:, :]))
            done(v.tensor_scalar(int_a[:, :], src_i[:, cols], 7, None, ALU.logical_shift_right))
            done(v.tensor_copy(src_hi[:, :], int_a[:, :]))
            dve.wait_ge(s_tr, 4)
            v.tensor_copy(ew[:, :], ring_ps[2][:, cols]).then_inc(s_ew, 1)

            dve.wait_ge(s_deg, 1)
            done(v.reciprocal(dinv[:, :], dinv[:, :]))
            dve.wait_ge(s_lx, 32)
            v.tensor_tensor(Xs[:, :, :], X[:, :, :], dinv[:, :].unsqueeze(2).to_broadcast([P, HB, D]),
                            ALU.mult).then_inc(s_xs, 1)
            dve.wait_ge(s_act, 1)
            v.tensor_tensor(Y[:, :, :], Xs[:, :, :], Xp[0][:, :, :], ALU.subtract).then_inc(s_xs, 1)
            dve.wait_ge(s_act, 2)
            v.tensor_tensor(Xp[2][:, :, :], Y[:, :, :], Xp[1][:, :, :], ALU.subtract).then_inc(s_xs, 1)

            def next_windows():
                v.tensor_scalar(relw[:, :], relw[:, :], float(-WIN), None, ALU.add)
                loop.done(v.tensor_scalar(base_row[:, :], base_row[:, :], float(WIN), float(LAST_BASE),
                                          ALU.add, ALU.min))
                loop.done(v.tensor_copy(base_i[:, :], base_row[:, :]))

            def starts(tile, n):
                return nc.values_load_multi_w_load_instructions(
                    base_i[0:1, bass.ds(tile, n)], engines=[mybir.EngineType.DVE], min_val=0, max_val=LAST_BASE,
                    skip_runtime_bounds_check_because="clamped to 0..LAST_BASE when made")[1]

            def one_hots(m, b, beside=None):
                dve.wait_ge(s_stage0, m + 1)
                dve.wait_ge(s_cnt_mm, (m + 1) * BATCH)
                for j in range(BATCH):
                    q = b * BATCH + j
                    v.tensor_scalar(oh_src[:, q, :], iota_row[:, :], stage0[:, b, 1, j:j + 1], None, ALU.is_equal)
                    v.tensor_scalar(oh_key[:, q, :], iota_keys[:, :], stage0[:, b, 0, j:j + 1], None,
                                    ALU.is_equal).then_inc(s_oh, 1)
                    if beside:
                        beside(j)

            def add_batch(w, i, b):
                m = w * NB + i * 2 + b
                at = []
                for j0 in range(0, BATCH, HALF):
                    at += starts((i * 2 + b) * BATCH + j0, HALF)
                dve.wait_ge(s_zadd, m + 2)
                loop.restart()
                dve.wait_ge(s_z, m + 3)

                def add(j):
                    if j > 0:
                        dve.wait_ge(s_loop, j)
                    ins = v.tensor_tensor(sum0[:, bass.ds(at[j], WIN)], sum0[:, bass.ds(at[j], WIN)],
                                          z_ps[b][:, j * WIN:(j + 1) * WIN], ALU.add)
                    ins.then_inc(s_loop if j < BATCH - 1 else s_zadd, 1)
                return add

            dve.sem_inc(s_zadd, 2)
            dve.sem_inc(s_oh, OHS)
            dve.wait_ge(s_xTc, -(-HB // 4))
            with dve.Fori(0, n_pass) as w:
                loop.restart()
                loop.done(v.tensor_scalar(valid[:, :], relw[:, :], 0.0, None, ALU.is_ge))
                v.scalar_tensor_tensor(keylo[:, 0, :], src_hi[:, :], float(WIN), relw[:, :], ALU.mult, ALU.add)
                loop.done(v.scalar_tensor_tensor(valid[:, :], relw[:, :], float(WIN - 1), valid[:, :], ALU.is_le,
                                                 ALU.mult))
                v.scalar_tensor_tensor(keylo[:, 0, :], keylo[:, 0, :], 1.0, valid[:, :], ALU.add,
                                       ALU.mult).then_inc(s_key, 1)
                one_hots(w * NB, 0)
                one_hots(w * NB + 1, 1)
                one_hots(w * NB + 2, 0)
                with dve.Fori(0, (NB - 4) // 2) as i:
                    one_hots(w * NB + i * 2 + 3, 1, add_batch(w, i, 0))
                    one_hots(w * NB + i * 2 + 4, 0, add_batch(w, i, 1))
                one_hots(w * NB + NB - 1, 1, add_batch(w, (NB - 4) // 2, 0))
                for m in range(NB - 3, NB):
                    add = add_batch(w, m // 2, m % 2)
                    for j in range(BATCH):
                        add(j)
                dve.wait_ge(s_zadd, w * NB + (NB + 2))
                loop.restart()
                next_windows()
            dve.wait_ge(s_zadd, n_pass * NB + 2)

            dve.wait_ge(s_lw, 16 * (6 + GROUPS))
            for h in range(HB):
                dve.wait_ge(s_y, h + 1)
                v.scalar_tensor_tensor(Y[:, h, :], ring_ps[h % 4][:, 0:D], dinv[:, h:h + 1], b0_all[:, :],
                                       ALU.mult, ALU.add).then_inc(s_yev, 1)
            dve.wait_ge(s_y, HB + 1)
            done(v.tensor_scalar(bn_a[:, :], misc[0][:, 0:D], 1.0 / N, None, ALU.mult))
            v.tensor_tensor(Y[:, :, :], Y[:, :, :], bn_a[:, :].unsqueeze(1).to_broadcast([P, HB, D]),
                            ALU.subtract).then_inc(s_bn, 1)
            v.tensor_tensor(X[:, :, :], X[:, :, :], beta_all[:, :].unsqueeze(1).to_broadcast([P, HB, D]), ALU.add)
            dve.wait_ge(s_y, HB + 2)
            dve.sem_inc(s_bn, 1)
            dve.wait_ge(s_act, 2 + -(-HB // 4) + 2)
            done(v.reciprocal(bn_b[:, :], bn_b[:, :]))
            done(v.tensor_tensor(bn_b[:, :], bn_b[:, :], gamma_all[:, :], ALU.mult))
            done(v.tensor_tensor(Y[:, :, :], Y[:, :, :], bn_b[:, :].unsqueeze(1).to_broadcast([P, HB, D]), ALU.mult))
            done(v.tensor_tensor(Y[:, :, :], Y[:, :, :], X[:, :, :], ALU.add))
            for h in range(HB):
                last = v.bn_stats(stats[:, h, :], Y[:, h, :])
            done(last)
            for h in range(HB):
                last = v.bn_aggr(mv[:, h, :], stats[:, h, :])
            last.then_inc(s_bn, 1)
            dve.wait_ge(s_act, 2 + -(-HB // 4) + 3)
            done(v.reciprocal(rstd[:, :], rstd[:, :]))
            for h in range(HB):
                last = v.tensor_scalar(Xs[:, h, :], Y[:, h, :], mv[:, h, 0:1], rstd[:, h:h + 1],
                                       ALU.subtract, ALU.mult)
            last.then_inc(s_x1, 1)

            dve.wait_ge(s_coef, 1)
            dve.wait_ge(s_act, 2 + -(-HB // 4) + 4)
            v.tensor_copy(relw[:, :], rel[:, :])
            v.tensor_copy(base_row[:, :], base_row0[:, :])
            done(v.tensor_copy(base_i[:, :], base_row0[:, :]))
            dve.sem_inc(s_add, 1)

            def coefficients(w, i):
                for b in range(2):
                    t0 = i * RING + b * HALF
                    dve.wait_ge(s_mm, w * TILES + t0 + HALF)
                    v.tensor_tensor(
                        S[:, b * HALF:(b + 1) * HALF, :, :],
                        ohw[:, bass.ds(t0, HALF), :].unsqueeze(2).to_broadcast([P, HALF, K, WIN]),
                        coef[:, bass.ds(t0, HALF), :].unsqueeze(3).to_broadcast([P, HALF, K, WIN]),
                        ALU.mult).then_inc(s_S, 1)

            def add_ring(w, i):
                ring = w * (TILES // RING) + i
                at = starts(i * RING, HALF) + starts(i * RING + HALF, HALF)
                dve.wait_ge(s_add, ring + 1)
                loop.restart()
                dve.wait_ge(s_r, ring + 2)
                for j in range(RING):
                    if j > 0:
                        dve.wait_ge(s_loop, j)
                    v.tensor_tensor(sum1[:, bass.ds(at[j], WIN)], sum1[:, bass.ds(at[j], WIN)],
                                    z_ps[0][:, j * WIN:(j + 1) * WIN],
                                    ALU.add).then_inc(s_loop if j < RING - 1 else s_add, 1)

            with dve.Fori(0, n_pass) as w:
                v.tensor_tensor(ohw[:, :, :], relw[:, :].unsqueeze(2).to_broadcast([P, TILES, WIN]),
                                iota_win[:, :].unsqueeze(1).to_broadcast([P, TILES, WIN]),
                                ALU.is_equal).then_inc(s_ohw, 1)
                dve.wait_ge(s_ohw, w + 1)
                dve.sem_inc(s_turn)
                coefficients(w, 0)
                with dve.Fori(0, TILES // RING - 1) as i:
                    coefficients(w, i + 1)
                    add_ring(w, i)
                add_ring(w, TILES // RING - 1)
                dve.wait_ge(s_add, (w + 1) * (TILES // RING) + 1)
                loop.restart()
                next_windows()

            for q in range(-(-HB // 4)):
                hs = range(4 * q, min(4 * q + 4, HB))
                for h in hs:
                    dve.wait_ge(s_tfin, h + 1)
                    v.scalar_tensor_tensor(Y[:, h, :], ring_ps[h % 4][:, 0:P], 0.0, Xs[:, h, :], ALU.max,
                                           ALU.add).then_inc(s_fin, 1)
                for h in hs:
                    dve.wait_ge(s_fin, h + 1)
                    last = v.bn_stats(stats[:, h, :], Y[:, h, :])
                done(last)
                for h in hs:
                    last = v.bn_aggr(mv[:, h, :], stats[:, h, :])
                last.then_inc(s_fev, 1)
                dve.wait_ge(s_act, 2 + -(-HB // 4) + 4 + q + 1)
                done(v.reciprocal(rstd[:, hs.start:hs.stop], rstd[:, hs.start:hs.stop]))
                for h in hs:
                    v.tensor_scalar(Y[:, h, :], Y[:, h, :], mv[:, h, 0:1], rstd[:, h:h + 1],
                                    ALU.subtract, ALU.mult).then_inc(s_outr, 1)


_INS = ['x', 'src', 'dst', 'edge_type_32', 'edge_weight1', 'L0_gnn_W', 'L0_gnn_b', 'L0_gnn_gamma',
        'L0_gnn_beta', 'L1_gnn_weight', 'L1_gnn_w_comp', 'L1_gnn_bias_param']
_OUTS = [((3125, 128), 'float32')]


def kernel(**inputs):
    import numpy as _np
    import concourse.bacc as _bacc
    from concourse import mybir as _mybir
    from concourse.bass_utils import run_bass_kernel_spmd as _run

    nc = _bacc.Bacc("TRN2", target_bir_lowering=False, num_devices=1)
    arrays, args = {}, []
    for name in _INS:
        a = _np.ascontiguousarray(inputs[name])
        arrays[f"in_{name}_dram"] = a
        args.append(nc.dram_tensor(f"in_{name}_dram", a.shape, _mybir.dt.from_np(a.dtype), kind="ExternalInput").ap())
    for i, (shape, dtype) in enumerate(_OUTS):
        dt = _mybir.dt.from_np(_np.dtype(dtype))
        args.append(nc.dram_tensor(f"out_{i}_dram", shape, dt, kind="ExternalOutput").ap())
    args.append(nc.dram_tensor("x1_dram", _OUTS[0][0], _mybir.dt.float32, kind="Internal").ap())
    gnn_kernel(nc, *args)
    r = _run(nc, [arrays], core_ids=[0])
    got = tuple(r.results[0][f"out_{i}_dram"] for i in range(len(_OUTS)))
    return got[0]
```

```python
from contextlib import ExitStack

import concourse.bass as bass
import numpy as np
from concourse import mybir

F32 = mybir.dt.float32
BF16 = mybir.dt.bfloat16
FP16 = mybir.dt.float16
I32 = mybir.dt.int32
ALU = mybir.AluOpType
ACT = mybir.ActivationFunctionType
AX_X = mybir.AxisListType.X

P = 128
EPS = 1e-5


def gnn_kernel(nc, x, src, dst, etype, eweight, w0, b0, gamma, beta, w1, wcomp, b1, out, xs_dram, x1_dram):
    N, D = x.shape
    E = src.shape[0]
    K = w1.shape[0]
    R = wcomp.shape[0]
    assert D == P
    UNIT = 32
    TILES = -(-E // (UNIT * P)) * UNIT
    HB = -(-N // P)
    NTAIL = N - (HB - 1) * P
    NPAD = HB * P
    WIN = 12
    LAST_BASE = NPAD - WIN
    PASSES = -(-N // WIN) + 1
    KEYS = HB * WIN
    BATCH = 18
    GB = 8
    NB = TILES // (BATCH + GB)
    SPAN = BATCH + GB
    BW = BATCH * WIN
    TG = -(-TILES // P)
    TLAST = TILES - (TG - 1) * P
    FULL_ROWS = E // P - (TG - 1) * P
    REST = E % P
    HALF = 8
    RING = 2 * HALF
    QUAD = 4
    NQ = RING // QUAD
    RINGS = TILES // RING
    PICK = HALF - 1
    STEPS = RINGS + 1
    GROUPS = P // R
    GT = TILES // GROUPS
    CT = 8
    CHUNKS = GT // CT
    CW = CT * GROUPS * K
    TYPE_SLOTS = 3
    EARLY = 7
    X1_PARTS = 3
    QH = -(-HB // 4)
    assert HB == 4 * (QH - 1) + 1
    assert NQ == 4 and RINGS * RING == TILES and (TILES - HALF) * P <= E
    assert NB * SPAN == TILES and NB % 2 == 0
    assert GT % CT == 0 and CW <= 512 and TLAST == 32 and 0 < REST

    with ExitStack() as ctx:
        def sb(name, shape, dt):
            return ctx.enter_context(nc.sbuf_tensor(name, shape, dt))

        def ps(name, shape, dt=F32):
            return ctx.enter_context(nc.psum_tensor(name, shape, dt))

        def sem(name):
            return ctx.enter_context(nc.semaphore(name))

        ident = sb("ident", [P, P], F32)
        ones = sb("ones", [P, P], F32)
        iota_row = sb("iota_row", [P, P], FP16)
        iota_keys = sb("iota_keys", [P, KEYS], FP16)
        iota_blk = sb("iota_blk", [P, HB], F32)
        iota_win = sb("iota_win", [P, WIN], F32)
        win_ends = sb("win_ends", [1, PASSES], F32)
        part_id = sb("part_id", [P, 1], I32)
        node_id = sb("node_id", [P, HB], F32)
        rel_id = sb("rel_id", [P, 1], F32)
        X = sb("X", [P, HB, D], F32)
        W0 = sb("W0", [P, D], F32)
        W1 = sb("W1", [P, K, D], F32)
        beta_all = sb("beta_all", [P, D], F32)
        b0_col = sb("b0_col", [P, 1], F32)
        gamma_col = sb("gamma_col", [P, 1], F32)
        b1_col = sb("b1_col", [P, 1], F32)
        wblk = sb("wblk", [P, GROUPS, K], F32)
        wparts = sb("wparts", [P, 3, GROUPS * K], BF16)
        ew_t = sb("ew_t", [P, TG, P], F32)
        base_t = sb("base_t", [P, TG], F32)
        max_t = sb("max_t", [P, TG], F32)
        rel = sb("rel", [P, TILES], F32)
        relw = sb("relw", [P, TILES], F32)
        ew = sb("ew", [P, TILES], F32)
        src_i = sb("src_i", [P, TILES + RING], I32)
        ohw = sb("ohw", [P, TILES, WIN], BF16)
        zeros = sb("zeros", [P, P], BF16)
        base_row0 = sb("base_row0", [1, TG * P], F32)
        coef = sb("coef", [P, TILES, K], F32)
        base_row = sb("base_row", [1, TG * P], F32)
        span_row = sb("span_row", [1, TG * P], F32)
        base_i = sb("base_i", [1, TG * P], I32)
        span_max = sb("span_max", [1, 1], F32)
        npass_f = sb("npass_f", [1, 1], F32)
        npass_i = sb("npass_i", [1, 1], I32)
        dinv = sb("dinv", [P, HB], F32)
        Xs_all = sb("Xs", [P, HB * D], F32)
        Xs = Xs_all[:, :].rearrange("p (h f) -> p h f", h=HB)
        OHS = 2 * BATCH
        stage0 = sb("stage0", [P, 2, 2, BATCH], F32)
        sum0 = sb("sum0", [P, NPAD], F32)
        late = sb("late", [P, NPAD + K * RING * WIN], F32)
        sum1 = late[:, 0:NPAD]

        def inside(space, at, dt, *dims):
            words = -(-int(np.prod(dims)) * (4 if dt in (F32, I32) else 2) // 4)
            assert at + words <= space.shape[1]
            names = "abcd"[:len(dims)]
            view = space[:, at:at + words].bitcast(dt).rearrange(
                f"p ({' '.join(names)}) -> p {' '.join(names)}", **dict(zip(names, dims)))
            return view, at + words

        Xparts = sb("Xparts", [P, HB, 3, D], BF16)
        Xp = [Xparts[:, :, i, :] for i in range(3)]
        G0w, at = inside(late, 0, F32, 2 * GB, 3 * D // 2)
        G0, at = inside(late, 0, BF16, 2 * GB, 3, D)
        idx0 = sb("idx0", [P, 2, GB], I32)
        ohw0 = sb("ohw0", [P, 2, GB, WIN], BF16)
        oh_src = sb("oh_src", [P, OHS, P], BF16)
        keys_room = sb("keys_room", [P, OHS * KEYS // 2], F32)
        oh_key, at = inside(keys_room, 0, BF16, OHS, KEYS)
        G, at = inside(keys_room, 0, F32, RING, D)
        pick_src, at = inside(keys_room, at, I32, RINGS, P)
        ITEMS = TG * WIN
        hist_lo = oh_key[:, :, :].rearrange("p s k -> p (s k)")[:, 0:ITEMS * P].rearrange("p (q n) -> p q n", n=P)
        Y_all = sb("Y", [P, HB * D], F32)
        Y = Y_all[:, :].rearrange("p (h f) -> p h f", h=HB)
        sum0b = Y_all[:, :]
        oh_pick, at = inside(sum0, 0, BF16, HB, P)
        hist_blk, at = inside(Y_all, 0, BF16, ITEMS, HB)
        rel_half = sb("rel_half", [P, TG * P], FP16)
        is_node, at = inside(sum0, 0, BF16, WIN, TG, P)
        room = sb("room", [P, max((TYPE_SLOTS + 2) * CT * P, BATCH * WIN * HB)], F32)
        types, at = inside(room, 0, I32, TYPE_SLOTS, CT * P)
        oh_type, at = inside(room, at, BF16, 2, CT * P)
        counts, at = inside(room, 0, BF16, 2, HB, BW)
        S, at = inside(room, 0, F32, RING, K, WIN)
        dst_ti, at = inside(Xs_all, 0, I32, TG, P)
        src_ti, at = inside(Xs_all, at, I32, TG, P)
        dst_t, at = inside(Xs_all, at, F32, TG, P)
        src_t, at = inside(Xs_all, at, F32, TG, P)
        rel_t, at = inside(Xs_all, at, F32, TG, P)
        idx = sb("idx", [P, 2, HALF], I32)
        tables = sb("tables", [P, 5 * (TILES + ITEMS)], F32)
        keylo, at = inside(tables, 0, F32, 2, TILES)
        src_hi, at = inside(tables, at, F32, TILES)
        valid, at = inside(tables, at, F32, TILES)
        int_a, at = inside(tables, at, I32, TILES)
        node_cnt, at = inside(tables, at, F32, ITEMS)
        node_i, at = inside(tables, at, I32, ITEMS)
        node_bits, at = inside(tables, at, I32, ITEMS)
        node_lo, at = inside(tables, at, F32, ITEMS)
        node_hi, at = inside(tables, at, F32, ITEMS)
        by_basis, at = inside(late, NPAD, F32, K, RING * WIN)
        stats = sb("stats", [P, HB, 6], F32)
        mv = sb("mv", [P, HB, 2], F32)
        rstd = sb("rstd", [P, HB], F32)
        shift = sb("shift", [P, HB], F32)
        bn_mv = sb("bn_mv", [P, 2], F32)
        bn_scale = sb("bn_scale", [P, 1], F32)
        bn_shift = sb("bn_shift", [P, 1], F32)
        eps_c = sb("eps_c", [P, 1], F32)

        ring_ps = [ps(f"ring_ps{i}", [P, 512]) for i in range(4)]
        z_ps = [ps(f"z_ps{i}", [P, 512]) for i in range(2)]
        misc = [ps(f"misc{i}", [P, 512]) for i in range(2)]
        coef_ps = [z_ps[0], ring_ps[3]]
        xT_ps = [misc[0], z_ps[1]]
        back_ps = [misc[0], misc[1], z_ps[0], z_ps[1]]

        s_iota = sem("s_iota")
        s_const = sem("s_const")
        s_pad = sem("s_pad")
        s_ldst = sem("s_ldst")
        s_lsrc = sem("s_lsrc")
        s_lew = sem("s_lew")
        s_lx = sem("s_lx")
        s_lw = sem("s_lw")
        s_types = [sem(f"s_types{i}") for i in range(TYPE_SLOTS)]
        s_dve = sem("s_dve")
        s_loop2 = sem("s_loop2")
        s_loop = sem("s_loop")
        s_tr = sem("s_tr")
        s_tab = sem("s_tab")
        s_prep = sem("s_prep")
        s_hist = sem("s_hist")
        s_histmm = sem("s_histmm")
        s_oht = sem("s_oht")
        s_cmm = sem("s_cmm")
        s_cev = sem("s_cev")
        s_deg = sem("s_deg")
        s_act = sem("s_act")
        s_xs = sem("s_xs")
        s_xT = sem("s_xT")
        s_xTc = sem("s_xTc")
        s_key = sem("s_key")
        s_stage0 = sem("s_stage0")
        s_oh = sem("s_oh")
        s_cnt_mm = sem("s_cnt_mm")
        s_cnt = sem("s_cnt")
        s_z = sem("s_z")
        s_zadd = sem("s_zadd")
        s_turn = sem("s_turn")
        s_y = sem("s_y")
        s_yev = sem("s_yev")
        s_bn = sem("s_bn")
        s_x1 = sem("s_x1")
        s_x1st = sem("s_x1st")
        s_stage1 = sem("s_stage1")
        s_g = [sem(f"s_g{i}") for i in range(RING)]
        s_S = sem("s_S")
        s_mm = sem("s_mm")
        s_add = sem("s_add")
        s_radd = sem("s_radd")
        s_fev = sem("s_fev")
        s_outr = sem("s_outr")
        s_out = sem("s_out")
        s_ohw = sem("s_ohw")
        s_relid = sem("s_relid")
        s_ew = sem("s_ew")
        s_coef = sem("s_coef")
        s_byb = sem("s_byb")
        s_r = sem("s_r")
        s_back = sem("s_back")
        s_relu = sem("s_relu")
        s_g0 = [sem(f"s_g0_{i}") for i in range(2 * GB)]
        s_stagei = sem("s_stagei")
        s_xsst = sem("s_xsst")
        s_zero = sem("s_zero")
        s_dbc = sem("s_dbc")
        s_stat = sem("s_stat")
        s_edges = sem("s_edges")
        s_lwc = sem("s_lwc")
        s_lpick = sem("s_lpick")
        s_x1p = sem("s_x1p")
        s_x1d = sem("s_x1d")
        s_ohpick = sem("s_ohpick")
        s_pick = sem("s_pick")
        s_picked = sem("s_picked")
        s_wparts = sem("s_wparts")
        s_merge = sem("s_merge")
        s_bnorm = sem("s_bnorm")
        s_dbcmm = sem("s_dbcmm")
        s_xbeta = sem("s_xbeta")
        s_froot = sem("s_froot")
        s_fshift = sem("s_fshift")

        def passes(eng):
            eng.wait_ge(s_prep, 1)
            return eng.value_load(npass_i[0:1, 0:1], min_val=1, max_val=PASSES)

        halves = (slice(0, (HB + 1) // 2), slice((HB + 1) // 2, HB))

        def four(q):
            hs = slice(4 * q, min(4 * q + 4, HB))
            return hs, slice(hs.start * P, hs.stop * P)

        def block_rows(h):
            return P if h < HB - 1 else NTAIL

        def edges_by_tile(a):
            full = (TG - 1) * P * P
            return (a[0:full].rearrange("(g t p) -> t g p", t=P, p=P),
                    a[full:full + FULL_ROWS * P].rearrange("(t p) -> t p", p=P),
                    a[full + FULL_ROWS * P:E].rearrange("(t p) -> t p", t=1))

        def load_types(eng, c):
            for g in range(GROUPS):
                e0 = (g * GT + c * CT) * P
                n = min(CT * P, E - e0)
                eng.dma_start(types[g * R:(g + 1) * R, c % TYPE_SLOTS, 0:n],
                              etype[e0:e0 + n].partition_broadcast(R)).then_inc(s_types[c % TYPE_SLOTS], 16)

        block = ctx.enter_context(nc.Block())

        @block.sync
        def _(sp):
            def load_edges(tile, a, signal):
                main, rows, rest = edges_by_tile(a)
                sp.dma_start(tile[:, 0:TG - 1, :], main).then_inc(signal, 16)
                sp.dma_start(tile[0:FULL_ROWS, TG - 1, :], rows).then_inc(signal, 16)
                sp.dma_start(tile[FULL_ROWS:FULL_ROWS + 1, TG - 1, 0:REST], rest).then_inc(signal, 16)

            sp.wait_ge(s_pad, 2)
            load_edges(dst_ti, dst, s_ldst)
            load_edges(src_ti, src, s_lsrc)
            load_edges(ew_t, eweight.rearrange("e o -> (e o)"), s_lew)
            for c in range(TYPE_SLOTS, CHUNKS):
                sp.wait_ge(s_oht, c - TYPE_SLOTS + 1)
                load_types(sp, c)
            words = Xparts[:, :, :, :].rearrange("p h i f -> p h (i f)").bitcast(F32)
            sp.wait_ge(s_act, 4)
            sp.wait_ge(s_xs, 5)
            mid = halves[0].stop
            sp.dma_start(xs_dram[0:mid * P, :].rearrange("(h p) f -> p h f", p=P),
                         words[:, 0:mid, :]).then_inc(s_xsst, 16)
            sp.wait_ge(s_xs, 6)
            sp.dma_start(xs_dram[mid * P:(HB - 1) * P, :].rearrange("(h p) f -> p h f", p=P),
                         words[:, mid:HB - 1, :]).then_inc(s_xsst, 16)
            sp.dma_start(xs_dram[(HB - 1) * P:N, :], words[0:NTAIL, HB - 1, :]).then_inc(s_xsst, 16)
            sp.wait_ge(s_merge, QH)
            e0, stride = PICK * P, RING * P
            sp.dma_start(pick_src[:, 0:RINGS - 1, :],
                         src[e0:e0 + (RINGS - 1) * stride].rearrange("(r x) -> r x", x=stride)[:, 0:P]
                         .partition_broadcast(P)).then_inc(s_lpick, 16)
            e0 += (RINGS - 1) * stride
            sp.dma_start(pick_src[:, RINGS - 1, :], src[e0:e0 + P].partition_broadcast(P)).then_inc(s_lpick, 16)
            for part in range(X1_PARTS):
                h0, h1 = part * (HB - 1) // X1_PARTS, (part + 1) * (HB - 1) // X1_PARTS
                sp.wait_ge(s_x1, h1)
                sp.dma_start(x1_dram[h0 * P:h1 * P, :].rearrange("(h p) f -> p h f", p=P),
                             Xs[:, h0:h1, :]).then_inc(s_x1st, 16)
            sp.wait_ge(s_x1, HB)
            sp.dma_start(x1_dram[(HB - 1) * P:N, :], Xs[0:NTAIL, HB - 1, :]).then_inc(s_x1st, 16)
            for h in range(HB):
                sp.wait_ge(s_outr, h + 1)
                n = block_rows(h)
                sp.dma_start(out[h * P:h * P + n, :], Y[0:n, h, :]).then_inc(s_out, 16)
            sp.wait_ge(s_out, 16 * HB)

        @block.gpsimd
        def _(pool):
            g = nc.gpsimd
            g.memset(wblk[:, :, :], 0.0).then_inc(s_pad, 1)
            g.memset(dst_ti[:, TG - 1, :], -1)
            g.memset(src_ti[:, TG - 1, :], 0)
            g.memset(ew_t[:, TG - 1, :], 0.0).then_inc(s_pad, 1)
            g.memset(types[:, :, :], 0).then_inc(s_pad, 1)
            g.memset(X[:, HB - 1, :], 0.0).then_inc(s_pad, 1)
            g.memset(ones[:, :], 1.0)
            g.memset(zeros[:, :], 0.0)
            g.memset(ident[:, :], 0.0).then_inc(s_iota, 1)
            pool.wait_ge(s_iota, 1)
            g.affine_select(out=ident[:, :], in_=ident[:, :], compare_op=ALU.not_equal, fill=1.0, base=0,
                            pattern=[[-1, P]], channel_multiplier=1)
            g.memset(eps_c[:, :], EPS)
            imprecise = dict(allow_small_or_imprecise_dtypes=True)
            g.iota(iota_row[:, :], [[1, P]], base=0, channel_multiplier=0, **imprecise)
            g.iota(iota_keys[:, :], [[1, KEYS]], base=1, channel_multiplier=0, **imprecise)
            g.iota(node_id[:, :], [[P, HB]], base=0, channel_multiplier=1, **imprecise)
            g.iota(iota_blk[:, :], [[1, HB]], base=0, channel_multiplier=0, **imprecise)
            g.iota(iota_win[:, :], [[1, WIN]], base=0, channel_multiplier=0, **imprecise)
            g.iota(win_ends[:, :], [[WIN, PASSES]], base=WIN, channel_multiplier=0, **imprecise)
            g.iota(part_id[:, :], [[0, 1]], base=0, channel_multiplier=1).then_inc(s_const, 1)

            pool.wait_ge(s_lwc, 16 * GROUPS)
            rest = wblk[:, :, :].rearrange("p g k -> p (g k)")
            for k in range(3):
                g.tensor_copy(wparts[:, k, :], rest).then_inc(s_wparts, 1)
                pool.wait_ge(s_wparts, 2 * k + 1)
                if k < 2:
                    g.tensor_tensor(rest, rest, wparts[:, k, :], ALU.subtract).then_inc(s_wparts, 1)
                    pool.wait_ge(s_wparts, 2 * k + 2)
            pool.wait_ge(s_relid, 1)
            for c in range(CHUNKS):
                pool.wait_ge(s_types[c % TYPE_SLOTS], 16 * GROUPS * (c // TYPE_SLOTS + 1))
                if c >= 2:
                    pool.wait_ge(s_cmm, c - 1)
                g.tensor_scalar(oh_type[:, c % 2, :], types[:, c % TYPE_SLOTS, :], rel_id[:, :], None,
                                ALU.is_equal).then_inc(s_oht, 1)

            n_pass = passes(pool)
            def stage_keys(w, m, b):
                pool.wait_ge(s_oh, (w * NB + m + 1) * BATCH)
                pool.sem_inc(s_turn)
                g.tensor_copy(stage0[:, b, :, :], keylo[:, :, bass.ds(m * SPAN, BATCH)]).then_inc(s_stage0, 1)

            def gather0(w, m, b):
                pool.wait_ge(s_stagei, w * NB + m + 1)
                pool.sem_inc(s_turn)
                for j in range(GB):
                    q = b * GB + j
                    g.indirect_dma_start(G0w[:, q, :], None, xs_dram[:, :],
                                         bass.IndirectOffsetOnAxis(ap=idx0[:, b, j:j + 1], axis=0)
                                         ).then_inc(s_g0[q], 16)

            pool.wait_ge(s_key, 1)
            stage_keys(0, 0, 0)
            stage_keys(0, 1, 1)
            pool.wait_ge(s_xs, 6)
            g.memset(sum0b, 0.0).then_inc(s_zero, 1)
            with pool.Fori(0, n_pass) as w:
                pool.wait_ge(s_xsst, 48)
                pool.sem_inc(s_turn)
                with pool.Fori(0, NB // 2 - 1) as i:
                    for b in range(2):
                        gather0(w, i * 2 + b, b)
                        stage_keys(w, i * 2 + (2 + b), b)
                gather0(w, NB - 2, 0)
                gather0(w, NB - 1, 1)
                pool.wait_ge(s_key, w + 2)
                pool.sem_inc(s_turn)
                stage_keys(w + 1, 0, 0)
                stage_keys(w + 1, 1, 1)

            pool.wait_ge(s_xs, 2)
            pool.wait_ge(s_lw, 16 * 6)
            g.tensor_tensor(X[:, :, :], X[:, :, :], beta_all[:, :].unsqueeze(1).to_broadcast([P, HB, D]),
                            ALU.add).then_inc(s_xbeta, 1)

            pool.wait_ge(s_cev, CHUNKS)
            pool.wait_ge(s_ew, 1)
            g.tensor_tensor(coef[:, :, :], coef[:, :, :], ew[:, :].unsqueeze(2).to_broadcast([P, TILES, K]),
                            ALU.mult).then_inc(s_coef, 1)

            pool.wait_ge(s_x1st, 16 * (X1_PARTS + 1))
            with pool.Fori(0, n_pass) as w:
                with pool.Fori(0, TILES // RING) as i:
                    for b in range(2):
                        pool.wait_ge(s_stage1, w * (TILES // HALF) + i * 2 + b + 1)
                        pool.sem_inc(s_turn)
                        for j in range(HALF):
                            q = b * HALF + j
                            if q == PICK:
                                continue
                            g.indirect_dma_start(G[:, q, :], None, x1_dram[:, :],
                                                 bass.IndirectOffsetOnAxis(ap=idx[:, b, j:j + 1], axis=0)
                                                 ).then_inc(s_g[q], 16)

        @block.scalar
        def _(act):
            a = nc.scalar
            act.wait_ge(s_pad, 1)
            for g in range(GROUPS):
                act.dma_start(wblk[g * R:(g + 1) * R, g, :], wcomp).then_inc(s_lwc, 16)
            act.wait_ge(s_pad, 3)
            for c in range(TYPE_SLOTS):
                load_types(act, c)
            act.dma_start(X[:, 0:HB - 1, :],
                          x[0:(HB - 1) * P, :].rearrange("(h p) f -> p h f", p=P)).then_inc(s_lx, 16)
            act.dma_start(W0[:, :], w0).then_inc(s_lw, 16)
            act.dma_start(W1[:, :, :], w1.rearrange("k f o -> f k o")).then_inc(s_lw, 16)
            act.dma_start(beta_all[:, :], beta.partition_broadcast(P)).then_inc(s_lw, 16)
            with nc.allow_non_contiguous_dma("three vectors, once"):
                for vec, tile in ((b0, b0_col), (gamma, gamma_col), (b1, b1_col)):
                    act.dma_start(tile[:, :], vec.rearrange("(o u) -> o u", u=1)).then_inc(s_lw, 16)
            act.wait_ge(s_pad, 4)
            act.dma_start(X[0:NTAIL, HB - 1, :], x[(HB - 1) * P:N, :]).then_inc(s_lx, 16)

            def w_out(chunks):
                for c in chunks:
                    act.wait_ge(s_cmm, c + 1)
                    part = slice(c * CT, (c + 1) * CT)
                    a.copy(coef[:, :, :].rearrange("p (g t) k -> p g t k", g=GROUPS)[:, :, part, :],
                           coef_ps[c % 2][:, 0:CW].rearrange("p (t g k) -> p g t k", g=GROUPS, k=K)
                           ).then_inc(s_cev, 1)

            act.wait_ge(s_tr, 3)
            a.copy(relw[:, :], ring_ps[0][:, 0:TILES])
            a.copy(rel[:, :], ring_ps[0][:, 0:TILES]).then_inc(s_edges, 1)
            a.copy(src_i[:, TILES:TILES + RING], ring_ps[1][:, 0:RING]).then_inc(s_edges, 1)
            a.copy(src_i[:, 0:TILES], ring_ps[1][:, 0:TILES]).then_inc(s_edges, 1)
            act.wait_ge(s_tr, 4)
            a.copy(ew[:, :], ring_ps[2][:, 0:TILES]).then_inc(s_ew, 1)
            w_out(range(EARLY))
            n_pass = passes(act)
            act.wait_ge(s_histmm, n_pass * ITEMS + ITEMS)
            a.activation(dinv[:, :], misc[1][:, 0:HB], ACT.Sqrt, bias=ones[:, 0:1]).then_inc(s_deg, 1)
            w_out(range(EARLY, EARLY + 1))
            for part in range(2):
                for half, hs in enumerate(halves):
                    act.wait_ge(s_xs, part * 2 + half + 1)
                    a.copy(Xp[part][:, hs, :], (Xs, Y)[part][:, hs, :]).then_inc(s_act, 1)
                if part == 0:
                    w_out(range(EARLY + 1, CHUNKS - 1))
            for q in range(QH):
                hs, cols = four(q)
                act.wait_ge(s_xT, q + 1)
                a.copy(sum0[:, cols], xT_ps[q % 2][:, 0:cols.stop - cols.start]).then_inc(s_xTc, 1)
            w_out(range(CHUNKS - 1, CHUNKS))

            act.sem_inc(s_cnt, 4)
            def stage_tiles(w, m, b):
                act.wait_ge(s_z, w * NB + m + 1)
                at = m * SPAN + BATCH
                a.copy(idx0[:, b, :], src_i[:, bass.ds(at, GB)])
                a.copy(ohw0[:, b, :, :], ohw[:, bass.ds(at, GB), :]).then_inc(s_stagei, 1)

            def counts_out(w, m, b):
                act.wait_ge(s_z, w * NB + m + 1)
                for j in range(BATCH):
                    act.wait_ge(s_cnt_mm, (w * NB + m) * BATCH + (OHS + j + 1))
                    a.copy(counts[:, b, :, j * WIN:(j + 1) * WIN],
                           ring_ps[(b * BATCH + j) % 4][:, 0:KEYS].rearrange("p (h j) -> p h j", j=WIN)
                           ).then_inc(s_cnt, 1)

            with act.Fori(0, n_pass) as w:
                act.wait_ge(s_ohw, w + 1)
                stage_tiles(w, 0, 0)
                stage_tiles(w, 1, 1)
                counts_out(w, 0, 0)
                with act.Fori(0, NB // 2 - 1) as i:
                    counts_out(w, i * 2 + 1, 1)
                    stage_tiles(w, i * 2 + 2, 0)
                    counts_out(w, i * 2 + 2, 0)
                    stage_tiles(w, i * 2 + 3, 1)
                counts_out(w, NB - 1, 1)

            for q in range(QH):
                hs, cols = four(q)
                act.wait_ge(s_dbcmm, q + 1)
                a.copy(Xs_all[:, cols], ring_ps[q % 4][:, 0:cols.stop - cols.start]).then_inc(s_dbc, 1)
            act.wait_ge(s_lw, 16 * 6)
            for q in range(QH):
                hs, cols = four(q)
                act.wait_ge(s_yev, q + 1)
                a.activation(Y_all[:, cols], Y_all[:, cols], ACT.Relu, bias=b0_col[:, :]).then_inc(s_relu, 1)
            act.wait_ge(s_bn, 1)
            a.activation(bn_scale[:, :], bn_mv[:, 1:2], ACT.Sqrt, bias=eps_c[:, :]).then_inc(s_act, 1)
            act.wait_ge(s_bn, 2)
            for q in range(QH):
                hs, cols = four(q)
                a.activation(Y_all[:, cols], Y_all[:, cols], ACT.Identity, bias=bn_shift[:, :],
                             scale=bn_scale[:, :]).then_inc(s_bnorm, 1)

            def normalise(layer, to, made):
                for q in range(QH + 1):
                    if q < QH:
                        hs, cols = four(q)
                        act.wait_ge(s_fev, layer * QH + q + 1)
                        a.activation(rstd[:, hs], mv[:, hs, 1], ACT.Sqrt, bias=eps_c[:, :]).then_inc(s_froot, 1)
                    if q > 0:
                        act.wait_ge(s_fshift, layer * QH + q)
                        for h in range(4 * q - 4, min(4 * q, HB)):
                            a.activation(to[:, h, :], Y[:, h, :], ACT.Identity, bias=shift[:, h:h + 1],
                                         scale=rstd[:, h:h + 1]).then_inc(made, 1)

            normalise(0, Xs, s_x1)

            for b in range(2):
                a.copy(idx[:, b, :], src_i[:, b * HALF:(b + 1) * HALF]).then_inc(s_stage1, 1)
            act.wait_ge(s_x1, HB)
            act.wait_ge(s_xsst, 48)
            for part in range(2):
                for half, hs in enumerate(halves):
                    if part == 1:
                        act.wait_ge(s_x1d, half + 1)
                    a.copy(Xp[part][:, hs, :], (Xs, Y)[part][:, hs, :]).then_inc(s_x1p, 1)

            a.activation(sum1[:, :], Xs_all[:, :], ACT.Identity, bias=b1_col[:, :], scale=0.0).then_inc(s_act, 1)

            def picked_out(w, i):
                act.wait_ge(s_pick, w * RINGS + i + 2)
                act.wait_ge(s_mm, w * TILES + i * RING + HALF)
                a.copy(G[:, PICK, :], misc[0][:, 0:D]).then_inc(s_picked, 1)

            def sums_out(w, i):
                for q in range(NQ):
                    act.wait_ge(s_mm, w * TILES + i * RING + (RING + (q + 1) * QUAD))
                    if q == 0:
                        act.wait_ge(s_r, w * STEPS + i + 1)
                    a.copy(by_basis[:, :, q * QUAD * WIN:(q + 1) * QUAD * WIN].rearrange("p k (t j) -> p t k j", t=QUAD),
                           ring_ps[q][:, 0:QUAD * K * WIN].rearrange("p (t k j) -> p t k j", t=QUAD, k=K)
                           ).then_inc(s_byb, 1)
                    if q % 2 == 1:
                        t0 = i * RING + (RING + (q // 2) * HALF)
                        a.copy(idx[:, q // 2, :], src_i[:, bass.ds(t0, HALF)]).then_inc(s_stage1, 1)

            act.sem_inc(s_byb, NQ)
            act.sem_inc(s_picked, 1)
            with act.Fori(0, n_pass) as w:
                picked_out(w, 0)
                with act.Fori(0, RINGS - 1) as i:
                    sums_out(w, i)
                    picked_out(w, i + 1)
                sums_out(w, RINGS - 1)
            normalise(1, Y, s_outr)

        @block.tensor
        def _(pe):
            t = nc.tensor
            pe.wait_ge(s_const, 1)
            pe.wait_ge(s_tab, 1)
            for k, col in ((0, base_t), (1, max_t)):
                for g in range(TG):
                    last = t.matmul(misc[k][0:1, g * P:(g + 1) * P], col[:, g:g + 1], ident[:, :],
                                    start=True, stop=True)
            last.then_inc(s_tr, 1)
            pe.wait_ge(s_lew, 48)
            pe.sem_inc(s_histmm, ITEMS)
            for k, by_tile in enumerate((rel_t, src_t, ew_t)):
                for g in range(TG):
                    n = P if g < TG - 1 else TLAST
                    last = t.transpose(ring_ps[k][:, g * P:g * P + n], by_tile[0:n, g, :], ident[0:n, 0:n])
                last.then_inc(s_tr, 1)
            def w_of_edges(chunks):
                for c in chunks:
                    pe.wait_ge(s_oht, c + 1)
                    if c >= 2:
                        pe.wait_ge(s_cev, c - 1)
                    for j in range(CT):
                        for k in range(3):
                            last = t.matmul(coef_ps[c % 2][:, j * GROUPS * K:(j + 1) * GROUPS * K],
                                            oh_type[:, c % 2, j * P:(j + 1) * P], wparts[:, k, :],
                                            start=(k == 0), stop=(k == 2))
                    last.then_inc(s_cmm, 1)

            pe.wait_ge(s_wparts, 5)
            w_of_edges(range(EARLY))
            n_pass = passes(pe)
            t.matmul(misc[1][:, 0:HB], zeros[:, :], zeros[:, 0:HB], start=True, stop=False,
                     skip_group_check=True)
            with pe.Fori(0, n_pass) as w:
                for q in range(ITEMS):
                    pe.wait_ge(s_hist, w * ITEMS + (q + 1))
                    t.matmul(misc[1][:, 0:HB], hist_lo[:, q, :], hist_blk[:, q, :],
                             start=False, stop=False, skip_group_check=True).then_inc(s_histmm, 1)
            pe.sem_inc(s_cnt_mm, OHS)
            w_of_edges(range(EARLY, CHUNKS - 1))
            pe.wait_ge(s_xs, 2)
            for q in range(-(-HB // 4)):
                if q >= 2:
                    pe.wait_ge(s_xTc, q - 1)
                for j in range(min(4, HB - 4 * q)):
                    last = t.transpose(xT_ps[q % 2][:, j * P:(j + 1) * P], Xs[:, 4 * q + j, :], ident[:, :])
                last.then_inc(s_xT, 1)
            w_of_edges(range(CHUNKS - 1, CHUNKS))
            pe.wait_ge(s_xTc, -(-HB // 4))

            pe.sem_inc(s_z, 2)
            pe.sem_inc(s_mm, RING)

            def count(m, b, j):
                if j % 4 == 0:
                    pe.wait_ge(s_oh, m * BATCH + (OHS + min(j + 4, BATCH)))
                if j % 2 == 0:
                    pe.wait_ge(s_cnt, m * BATCH + (j + 2))
                t.matmul(ring_ps[(b * BATCH + j) % 4][:, 0:KEYS], oh_src[:, b * BATCH + j, :],
                         oh_key[:, b * BATCH + j, :], start=True, stop=True).then_inc(s_cnt_mm, 1)

            def aggregate(m, b, j, turn):
                if j == 0:
                    pe.wait_ge(s_cnt, m * BATCH + (4 + BATCH))
                    pe.wait_ge(s_zadd, m * 2 + 2)
                for q in range(j * 3 * HB // BATCH, (j + 1) * 3 * HB // BATCH):
                    last = t.matmul(z_ps[b][:, 0:BW], Xp[q % 3][:, q // 3, :], counts[:, b, q // 3, :],
                                    start=(q == 0), stop=(q == 3 * HB - 1))
                if j == 0:
                    pe.wait_ge(s_stagei, m + 1)
                if j < GB:
                    pe.wait_ge(s_g0[b * GB + j], turn * 16 + 16)
                    for k in range(3):
                        t.matmul(misc[b][:, j * WIN:(j + 1) * WIN], G0[:, b * GB + j, k, :], ohw0[:, b, j, :],
                                 start=(k == 0), stop=(k == 2))
                if j == BATCH - 1:
                    last.then_inc(s_z, 1)

            def step(m, b, turn):
                count(m + 1, 1 - b, 0)
                count(m + 1, 1 - b, 1)
                for j in range(BATCH):
                    aggregate(m, b, j, turn)
                    if j + 2 < BATCH:
                        count(m + 1, 1 - b, j + 2)

            pe.wait_ge(s_cev, CHUNKS)
            pe.wait_ge(s_ew, 1)
            pe.wait_ge(s_act, 4)
            pe.wait_ge(s_xs, 6)
            with pe.Fori(0, n_pass) as w:
                for j in range(BATCH):
                    count(w * NB, 0, j)
                with pe.Fori(0, NB // 2 - 1) as i:
                    step(w * NB + i * 2, 0, w * (NB // 2) + i)
                    step(w * NB + i * 2 + 1, 1, w * (NB // 2) + i)
                turn = w * (NB // 2) + (NB // 2 - 1)
                step(w * NB + NB - 2, 0, turn)
                for j in range(BATCH):
                    aggregate(w * NB + NB - 1, 1, j, turn)

            pe.wait_ge(s_cnt, n_pass * (NB * BATCH) + 4)
            for q in range(QH):
                hs, cols = four(q)
                if q >= 4:
                    pe.wait_ge(s_dbc, q - 3)
                for j in range(hs.stop - hs.start):
                    last = t.matmul(ring_ps[q % 4][:, j * P:(j + 1) * P],
                                    dinv[:, hs.start + j:hs.start + j + 1].to_broadcast([P, P]), ident[:, :],
                                    start=True, stop=True)
                last.then_inc(s_dbcmm, 1)
            pe.wait_ge(s_lw, 16 * 6)
            pe.wait_ge(s_dbc, QH)
            for q in range(QH):
                hs, cols = four(q)
                pe.wait_ge(s_merge, q + 1)
                if q >= 4:
                    pe.wait_ge(s_yev, q - 3)
                t.matmul(ring_ps[q % 4][:, 0:cols.stop - cols.start], W0[:, :], sum0[:, cols],
                         start=True, stop=True).then_inc(s_y, 1)

            def back(layer, by_feature, ready):
                for q in range(QH):
                    hs, cols = four(q)
                    n = layer * QH + q
                    if ready:
                        pe.wait_ge(ready, q + 1)
                    if n >= 4:
                        pe.wait_ge(s_radd, n - 3)
                    for j in range(hs.stop - hs.start):
                        at = cols.start + j * P
                        last = t.transpose(back_ps[n % 4][:, j * P:(j + 1) * P], by_feature[:, at:at + P], ident[:, :])
                    last.then_inc(s_back, 1)

            back(0, Y_all, s_bnorm)

            pe.sem_inc(s_r, 1)

            def pick(w, i, third):
                if third == 0:
                    pe.wait_ge(s_ohpick, w * RINGS + i + 1)
                    pe.wait_ge(s_picked, w * RINGS + i + 1)
                for n in range(third * HB, (third + 1) * HB):
                    last = t.matmul(misc[0][:, 0:D], oh_pick[:, n // 3, :], Xp[n % 3][:, n // 3, :],
                                    start=(n == 0), stop=(n == 3 * HB - 1))
                if third == 2:
                    last.then_inc(s_pick, 1)

            def tiles_of(w, i, quads, beside=False):
                for q in quads:
                    if q % 2 == 0:
                        pe.wait_ge(s_S, (w * RINGS + i) * 2 + (q // 2 + 1))
                    pe.wait_ge(s_byb, (w * RINGS + i) * NQ + (q + 1))
                    for j in range(q * QUAD, (q + 1) * QUAD):
                        if j == PICK:
                            pe.wait_ge(s_picked, w * RINGS + i + 2)
                        else:
                            pe.wait_ge(s_g[j], (w * RINGS + i) * 16 + 16)
                        at = (j - q * QUAD) * K * WIN
                        t.matmul(ring_ps[q][:, at:at + K * WIN], G[:, j, :],
                                 S[:, j, :, :].rearrange("p k j -> p (k j)"),
                                 start=True, stop=True).then_inc(s_mm, 1)
                    if beside and q > 0:
                        pick(w, i + 1, q - 1)

            def through_bases(w, i, step, quads, bank):
                pe.wait_ge(s_byb, (w * RINGS + i) * NQ + (NQ + quads.stop))
                pe.wait_ge(s_add, w * STEPS + step + 1)
                cols = slice(quads.start * QUAD * WIN, quads.stop * QUAD * WIN)
                for k in range(K):
                    last = t.matmul(z_ps[bank][:, cols], W1[:, k, :], by_basis[:, k, cols],
                                    start=(k == 0), stop=(k == K - 1))
                last.then_inc(s_r, 1)

            pe.sem_inc(s_pick, 1)
            pe.wait_ge(s_x1p, 4)
            pe.wait_ge(s_x1d, 4)
            whole, first, second = range(NQ), range(NQ // 2), range(NQ // 2, NQ)
            with pe.Fori(0, n_pass) as w:
                for third in range(3):
                    pick(w, 0, third)
                with pe.Fori(0, RINGS - 1) as i:
                    tiles_of(w, i, whole, beside=True)
                    through_bases(w, i, i, whole, 0)
                tiles_of(w, RINGS - 1, first)
                through_bases(w, RINGS - 1, RINGS - 1, first, 0)
                tiles_of(w, RINGS - 1, second)
                through_bases(w, RINGS - 1, RINGS - 1, second, 1)
            pe.wait_ge(s_add, n_pass * STEPS + 1)
            back(1, sum1, None)

        @block.vector
        def _(dve):
            v = nc.vector
            class Chain:

                def __init__(self, counter):
                    self.counter, self.n = counter, 0

                def restart(self):
                    dve.sem_inc(s_turn)
                    dve.sem_clear(self.counter)
                    self.n = 0

                def done(self, ins):
                    self.n += 1
                    ins.then_inc(self.counter, 1)
                    dve.wait_ge(self.counter, self.n)

            done = Chain(s_dve).done
            loop = Chain(s_loop)

            dve.wait_ge(s_const, 1)
            done(v.tensor_scalar(part_id[:, :], part_id[:, :], R - 1, None, ALU.bitwise_and))
            v.tensor_copy(rel_id[:, :], part_id[:, :]).then_inc(s_relid, 1)
            dve.wait_ge(s_ldst, 48)
            done(v.tensor_copy(dst_t[:, :, :], dst_ti[:, :, :]))
            done(v.tensor_scalar(rel_t[:, :, :], dst_t[:, :, :], 0.0, 8192.0, ALU.is_lt, ALU.mult))
            done(v.tensor_tensor(rel_t[:, :, :], rel_t[:, :, :], dst_t[:, :, :], ALU.add))
            v.tensor_reduce(max_t[:, :], dst_t[:, :, :], AX_X, ALU.max)
            done(v.tensor_reduce(base_t[:, :], rel_t[:, :, :], AX_X, ALU.min))
            done(v.tensor_scalar(base_t[:, :], base_t[:, :], float(LAST_BASE), None, ALU.min))
            for g in range(TG):
                last = v.tensor_scalar(rel_t[:, g, :], dst_t[:, g, :], base_t[:, g:g + 1], None, ALU.subtract)
            dve.wait_ge(s_lsrc, 48)
            last = v.tensor_copy(src_t[:, :, :], src_ti[:, :, :])
            last.then_inc(s_tab, 1)
            dve.wait_ge(s_tr, 1)
            v.tensor_copy(base_i[:, :], misc[0][0:1, :])
            v.tensor_copy(base_row0[:, :], misc[0][0:1, :])
            done(v.tensor_copy(base_row[:, :], misc[0][0:1, :]))
            done(v.tensor_tensor(span_row[:, :], misc[1][0:1, :], base_row[:, :], ALU.subtract))
            done(v.tensor_reduce(span_max[:, :], span_row[:, :], AX_X, ALU.max))
            done(v.tensor_scalar(win_ends[:, :], win_ends[:, :], span_max[:, :], None, ALU.is_le))
            done(v.tensor_reduce(npass_f[:, :], win_ends[:, :], AX_X, ALU.add))
            done(v.tensor_scalar(npass_f[:, :], npass_f[:, :], 1.0, None, ALU.add))
            v.tensor_copy(npass_i[:, :], npass_f[:, :]).then_inc(s_prep, 1)

            n_pass = passes(dve)
            dve.wait_ge(s_tr, 2)
            item = [P, TG, WIN]
            with dve.Fori(0, n_pass) as w:
                loop.restart()
                loop.done(v.tensor_copy(rel_half[:, :], rel_t[:, :, :].rearrange("p g e -> p (g e)")))
                for j in range(WIN):
                    last = v.tensor_scalar(is_node[:, j, :, :].rearrange("p g e -> p (g e)"), rel_half[:, :],
                                           float(j), None, ALU.is_equal)
                loop.done(last)
                n = P
                while n > 16:
                    n //= 2
                    loop.done(v.tensor_tensor(is_node[:, :, :, 0:n], is_node[:, :, :, 0:n], is_node[:, :, :, n:2 * n],
                                              ALU.add))
                loop.done(v.tensor_reduce(node_cnt[:, :].rearrange("p (g j) -> p j g", g=TG),
                                          is_node[:, :, :, 0:n], AX_X, ALU.add))
                loop.done(v.tensor_tensor(node_i[:, :].rearrange("p (g j) -> p g j", g=TG),
                                          base_t[:, :].unsqueeze(2).to_broadcast(item),
                                          iota_win[:, :].unsqueeze(1).to_broadcast(item), ALU.add))
                loop.done(v.tensor_scalar(node_bits[:, :], node_i[:, :], 127, None, ALU.bitwise_and))
                loop.done(v.tensor_copy(node_lo[:, :], node_bits[:, :]))
                loop.done(v.tensor_scalar(node_bits[:, :], node_i[:, :], 7, None, ALU.logical_shift_right))
                loop.done(v.tensor_copy(node_hi[:, :], node_bits[:, :]))
                dve.wait_ge(s_histmm, w * ITEMS + ITEMS)
                loop.done(v.tensor_tensor(hist_blk[:, :, :], node_hi[:, :].unsqueeze(2).to_broadcast([P, ITEMS, HB]),
                                          iota_blk[:, :].unsqueeze(1).to_broadcast([P, ITEMS, HB]), ALU.is_equal))
                loop.done(v.tensor_tensor(hist_blk[:, :, :], hist_blk[:, :, :],
                                          node_cnt[:, :].unsqueeze(2).to_broadcast([P, ITEMS, HB]), ALU.mult))
                for q in range(ITEMS):
                    v.tensor_scalar(hist_lo[:, q, :], iota_row[:, :], node_lo[:, q:q + 1], None,
                                    ALU.is_equal).then_inc(s_hist, 1)
                v.tensor_scalar(rel_t[:, :, :], rel_t[:, :, :], float(-WIN), None, ALU.add)
                loop.done(v.tensor_scalar(base_t[:, :], base_t[:, :], float(WIN), float(LAST_BASE), ALU.add, ALU.min))

            def next_windows():
                v.tensor_scalar(relw[:, :], relw[:, :], float(-WIN), None, ALU.add)
                loop.done(v.tensor_scalar(base_row[:, :], base_row[:, :], float(WIN), float(LAST_BASE),
                                          ALU.add, ALU.min))

            def next_starts():
                loop.done(v.tensor_copy(base_i[:, :], base_row[:, :]))

            def starts(tile, n):
                return nc.values_load_multi_w_load_instructions(
                    base_i[0:1, bass.ds(tile, n)], engines=[mybir.EngineType.DVE], min_val=0, max_val=LAST_BASE,
                    skip_runtime_bounds_check_because="clamped to 0..LAST_BASE when made")[1]

            def one_hots(m, b, beside=None):
                dve.wait_ge(s_stage0, m + 1)
                dve.wait_ge(s_cnt_mm, (m + 1) * BATCH)
                for j in range(BATCH):
                    q = b * BATCH + j
                    v.tensor_scalar(oh_src[:, q, :], iota_row[:, :], stage0[:, b, 1, j:j + 1], None, ALU.is_equal)
                    v.tensor_scalar(oh_key[:, q, :], iota_keys[:, :], stage0[:, b, 0, j:j + 1], None,
                                    ALU.is_equal).then_inc(s_oh, 1)
                    if beside:
                        beside(j)

            def add_batch(w, i, b):
                m = w * NB + i * 2 + b
                at = []
                for j0 in range(0, SPAN, SPAN // 2):
                    at += starts((i * 2 + b) * SPAN + j0, SPAN // 2)
                at, at_gathered = at[:BATCH], at[BATCH:]
                dve.wait_ge(s_zadd, 2 * m + 4)
                loop.restart()
                dve.sem_clear(s_loop2)
                dve.wait_ge(s_z, m + 3)
                chains = [(sum0[:, :], s_loop), (sum0b, s_loop2)]
                per_chain = (BATCH + GB) // 2
                so_far = [0, 0]

                def add(j):
                    for start, sums, there, c in ((at, z_ps, True, j % 2), (at_gathered, misc, j < GB, 1 - j % 2)):
                        if there:
                            total, counter = chains[c]
                            if so_far[c] > 0:
                                dve.wait_ge(counter, so_far[c])
                            so_far[c] += 1
                            v.tensor_tensor(total[:, bass.ds(start[j], WIN)], total[:, bass.ds(start[j], WIN)],
                                            sums[b][:, j * WIN:(j + 1) * WIN],
                                            ALU.add).then_inc(counter if so_far[c] < per_chain else s_zadd, 1)
                return add

            def window_one_hots(tiles):
                n = tiles.stop - tiles.start
                some = [P, NB, n, WIN]
                v.tensor_tensor(ohw[:, :, :].rearrange("p (m t) j -> p m t j", m=NB)[:, :, tiles, :],
                                relw[:, :].rearrange("p (m t) -> p m t", m=NB)[:, :, tiles]
                                .unsqueeze(3).to_broadcast(some),
                                iota_win[:, :].unsqueeze(1).unsqueeze(1).to_broadcast(some),
                                ALU.is_equal).then_inc(s_ohw, 1)

            def make_keys():
                loop.restart()
                loop.done(v.tensor_scalar(valid[:, :], relw[:, :], 0.0, None, ALU.is_ge))
                v.scalar_tensor_tensor(keylo[:, 0, :], src_hi[:, :], float(WIN), relw[:, :], ALU.mult, ALU.add)
                loop.done(v.scalar_tensor_tensor(valid[:, :], relw[:, :], float(WIN - 1), valid[:, :], ALU.is_le,
                                                 ALU.mult))
                v.scalar_tensor_tensor(keylo[:, 0, :], keylo[:, 0, :], 1.0, valid[:, :], ALU.add,
                                       ALU.mult).then_inc(s_key, 1)
                window_one_hots(slice(BATCH, SPAN))

            dve.wait_ge(s_deg, 1)
            done(v.reciprocal(dinv[:, :], dinv[:, :]))
            dve.wait_ge(s_lx, 32)
            for hs in halves:
                v.tensor_tensor(Xs[:, hs, :], X[:, hs, :],
                                dinv[:, hs].unsqueeze(2).to_broadcast([P, hs.stop - hs.start, D]),
                                ALU.mult).then_inc(s_xs, 1)
            dve.wait_ge(s_edges, 3)
            done(v.tensor_scalar(int_a[:, :], src_i[:, 0:TILES], 127, None, ALU.bitwise_and))
            done(v.tensor_copy(keylo[:, 1, :], int_a[:, :]))
            done(v.tensor_scalar(int_a[:, :], src_i[:, 0:TILES], 7, None, ALU.logical_shift_right))
            done(v.tensor_copy(src_hi[:, :], int_a[:, :]))
            for half, hs in enumerate(halves):
                dve.wait_ge(s_act, half + 1)
                v.tensor_tensor(Y[:, hs, :], Xs[:, hs, :], Xp[0][:, hs, :], ALU.subtract).then_inc(s_xs, 1)
            make_keys()
            for half, hs in enumerate(halves):
                dve.wait_ge(s_act, 2 + half + 1)
                v.tensor_tensor(Xp[2][:, hs, :], Y[:, hs, :], Xp[1][:, hs, :], ALU.subtract).then_inc(s_xs, 1)

            dve.sem_inc(s_zadd, 4)
            dve.sem_inc(s_oh, OHS)
            with dve.Fori(0, n_pass) as w:
                one_hots(w * NB, 0)
                one_hots(w * NB + 1, 1)
                one_hots(w * NB + 2, 0)
                dve.wait_ge(s_zero, 1)
                dve.wait_ge(s_xTc, QH)
                dve.sem_inc(s_turn)
                with dve.Fori(0, (NB - 4) // 2) as i:
                    one_hots(w * NB + i * 2 + 3, 1, add_batch(w, i, 0))
                    one_hots(w * NB + i * 2 + 4, 0, add_batch(w, i, 1))
                one_hots(w * NB + NB - 1, 1, add_batch(w, (NB - 4) // 2, 0))
                for m in range(NB - 3, NB):
                    add = add_batch(w, m // 2, m % 2)
                    for j in range(BATCH):
                        add(j)
                    if m == NB - 3:
                        dve.wait_ge(s_stage0, w * NB + NB)
                        dve.wait_ge(s_stagei, w * NB + NB)
                        dve.wait_ge(s_zadd, w * (2 * NB) + (2 * NB))
                        loop.restart()
                        next_windows()
                        make_keys()
                dve.wait_ge(s_zadd, w * (2 * NB) + (2 * NB + 4))
                loop.restart()
                next_starts()
            dve.wait_ge(s_zadd, n_pass * (2 * NB) + 4)
            for q in range(QH):
                hs, cols = four(q)
                v.tensor_tensor(sum0[:, cols], sum0[:, cols], sum0b[:, cols], ALU.add).then_inc(s_merge, 1)
            dve.wait_ge(s_merge, QH)

            for q in range(QH + 1):
                if q < QH:
                    hs, cols = four(q)
                    dve.wait_ge(s_dbc, q + 1)
                    dve.wait_ge(s_y, q + 1)
                    v.tensor_tensor(Y_all[:, cols], ring_ps[q % 4][:, 0:cols.stop - cols.start], Xs_all[:, cols],
                                    ALU.mult).then_inc(s_yev, 1)
                if q > 0:
                    hs, cols = four(q - 1)
                    dve.wait_ge(s_relu, q)
                    last = v.bn_stats(stats[:, q - 1, :], Y_all[:, cols.start:min(cols.stop, N)])
            done(last)
            v.bn_aggr(bn_mv[:, :], stats[:, 0:QH, :].rearrange("p q s -> p (q s)")).then_inc(s_bn, 1)
            dve.wait_ge(s_bn, 1)
            dve.wait_ge(s_act, 4 + 1)
            dve.wait_ge(s_lw, 16 * 6)
            done(v.reciprocal(bn_scale[:, :], bn_scale[:, :]))
            done(v.tensor_tensor(bn_scale[:, :], bn_scale[:, :], gamma_col[:, :], ALU.mult))
            v.scalar_tensor_tensor(bn_shift[:, :], bn_mv[:, 0:1], -1.0, bn_scale[:, :], ALU.mult,
                                   ALU.mult).then_inc(s_bn, 1)

            def residual(layer, add):
                for q in range(QH + 2):
                    n = layer * QH + q
                    if q < QH:
                        hs, cols = four(q)
                        dve.wait_ge(s_back, n + 1)
                        add(back_ps[n % 4][:, 0:cols.stop - cols.start].rearrange("p (h f) -> p h f", f=D),
                            hs).then_inc(s_radd, 1)
                    if 0 < q <= QH:
                        hs, cols = four(q - 1)
                        dve.wait_ge(s_stat, n)
                        for h in range(hs.start, hs.stop):
                            last = v.bn_aggr(mv[:, h, :], stats[:, h, :])
                        last.then_inc(s_fev, 1)
                    if q < QH:
                        hs, cols = four(q)
                        dve.wait_ge(s_radd, n + 1)
                        for h in range(hs.start, hs.stop):
                            last = v.bn_stats(stats[:, h, :], Y[:, h, :])
                        last.then_inc(s_stat, 1)
                    if q > 1:
                        hs, cols = four(q - 2)
                        dve.wait_ge(s_froot, n - 1)
                        dve.wait_ge(s_fev, n - 1)
                        done(v.reciprocal(rstd[:, hs], rstd[:, hs]))
                        v.scalar_tensor_tensor(shift[:, hs], mv[:, hs, 0], -1.0, rstd[:, hs], ALU.mult,
                                               ALU.mult).then_inc(s_fshift, 1)

            dve.wait_ge(s_xbeta, 1)
            residual(0, lambda ps_cols, hs: v.tensor_tensor(Y[:, hs, :], ps_cols, X[:, hs, :], ALU.add))

            def one_hot_of_sources(w, i):
                dve.wait_ge(s_pick, w * RINGS + i + 1)
                v.tensor_tensor(oh_pick[:, :, :], pick_src[:, bass.ds(i, 1), :].to_broadcast([P, HB, P]),
                                node_id[:, :].unsqueeze(2).to_broadcast([P, HB, P]),
                                ALU.is_equal).then_inc(s_ohpick, 1)

            dve.wait_ge(s_lpick, 32)
            dve.wait_ge(s_y, QH)
            one_hot_of_sources(0, 0)
            v.tensor_copy(relw[:, :], rel[:, :])
            v.tensor_copy(base_row[:, :], base_row0[:, :])
            done(v.tensor_copy(base_i[:, :], base_row0[:, :]))
            dve.sem_inc(s_add, 1)
            dve.wait_ge(s_x1, HB)
            for half, hs in enumerate(halves):
                dve.wait_ge(s_x1p, half + 1)
                v.tensor_tensor(Y[:, hs, :], Xs[:, hs, :], Xp[0][:, hs, :], ALU.subtract).then_inc(s_x1d, 1)
            for half, hs in enumerate(halves):
                dve.wait_ge(s_x1p, 2 + half + 1)
                v.tensor_tensor(Xp[2][:, hs, :], Y[:, hs, :], Xp[1][:, hs, :], ALU.subtract).then_inc(s_x1d, 1)
            def coefficients(w, i):
                for b in range(2):
                    t0 = i * RING + b * HALF
                    dve.wait_ge(s_mm, w * TILES + t0 + HALF)
                    v.tensor_tensor(
                        S[:, b * HALF:(b + 1) * HALF, :, :],
                        ohw[:, bass.ds(t0, HALF), :].unsqueeze(2).to_broadcast([P, HALF, K, WIN]),
                        coef[:, bass.ds(t0, HALF), :].unsqueeze(3).to_broadcast([P, HALF, K, WIN]),
                        ALU.mult).then_inc(s_S, 1)

            def add_tiles(w, i, step, tiles, bank):
                at = []
                for j0 in range(tiles.start, tiles.stop, HALF):
                    at += starts(i * RING + j0, HALF)
                dve.wait_ge(s_add, w * STEPS + step + 1)
                loop.restart()
                dve.wait_ge(s_r, w * STEPS + step + 2)
                for n, j in enumerate(tiles):
                    if n > 0:
                        dve.wait_ge(s_loop, n)
                    v.tensor_tensor(sum1[:, bass.ds(at[n], WIN)], sum1[:, bass.ds(at[n], WIN)],
                                    z_ps[bank][:, j * WIN:(j + 1) * WIN],
                                    ALU.add).then_inc(s_add if n == len(tiles) - 1 else s_loop, 1)

            dve.wait_ge(s_coef, 1)
            dve.wait_ge(s_act, 4 + 2)
            with dve.Fori(0, n_pass) as w:
                window_one_hots(slice(0, SPAN))
                dve.wait_ge(s_ohw, n_pass + w + 2)
                dve.sem_inc(s_turn)
                coefficients(w, 0)
                one_hot_of_sources(w, 1)
                with dve.Fori(0, RINGS - 2) as i:
                    coefficients(w, i + 1)
                    one_hot_of_sources(w, i + 2)
                    add_tiles(w, i, i, range(RING), 0)
                coefficients(w, RINGS - 1)
                add_tiles(w, RINGS - 2, RINGS - 2, range(RING), 0)
                dve.wait_ge(s_add, w * STEPS + (RINGS - 1) + 1)
                loop.restart()
                next_windows()
                one_hot_of_sources(w + 1, 0)
                add_tiles(w, RINGS - 1, RINGS - 1, range(HALF), 0)
                add_tiles(w, RINGS - 1, RINGS, range(HALF, RING), 1)
                dve.wait_ge(s_add, (w + 1) * STEPS + 1)
                loop.restart()
                next_starts()

            residual(1, lambda ps_cols, hs: v.scalar_tensor_tensor(Y[:, hs, :], ps_cols, 0.0, Xs[:, hs, :],
                                                                   ALU.max, ALU.add))


_INS = ['x', 'src', 'dst', 'edge_type_32', 'edge_weight1', 'L0_gnn_W', 'L0_gnn_b', 'L0_gnn_gamma',
        'L0_gnn_beta', 'L1_gnn_weight', 'L1_gnn_w_comp', 'L1_gnn_bias_param']
_OUTS = [((3125, 128), 'float32')]


def kernel(**inputs):
    import numpy as _np
    import concourse.bacc as _bacc
    from concourse import mybir as _mybir
    from concourse.bass_utils import run_bass_kernel_spmd as _run

    nc = _bacc.Bacc("TRN2", target_bir_lowering=False, num_devices=1)
    arrays, args = {}, []
    for name in _INS:
        a = _np.ascontiguousarray(inputs[name])
        arrays[f"in_{name}_dram"] = a
        args.append(nc.dram_tensor(f"in_{name}_dram", a.shape, _mybir.dt.from_np(a.dtype), kind="ExternalInput").ap())
    for i, (shape, dtype) in enumerate(_OUTS):
        dt = _mybir.dt.from_np(_np.dtype(dtype))
        args.append(nc.dram_tensor(f"out_{i}_dram", shape, dt, kind="ExternalOutput").ap())
    args.append(nc.dram_tensor("xs_dram", (3125, 192), _mybir.dt.float32, kind="Internal").ap())
    args.append(nc.dram_tensor("x1_dram", _OUTS[0][0], _mybir.dt.float32, kind="Internal").ap())
    gnn_kernel(nc, *args)
    r = _run(nc, [arrays], core_ids=[0])
    got = tuple(r.results[0][f"out_{i}_dram"] for i in range(len(_OUTS)))
    return got[0]
```
